# Optimizing a Trainium2 kernel written in Bass

```python
import numpy as np
import jax
import jax.numpy as jnp

def _softmax(x, axis=-1):
    return jax.nn.softmax(x, axis=axis)

def _gelu(x):
    return jax.nn.gelu(x, approximate=True)

def _silu(x):
    return jax.nn.silu(x)

def _sigmoid(x):
    return jax.nn.sigmoid(x)

def _layernorm(x, axis=-1, eps=1e-05):
    m = jnp.mean(x, axis=axis, keepdims=True)
    v = jnp.var(x, axis=axis, keepdims=True)
    return (x - m) / jnp.sqrt(v + eps)

def _scatter_add(tgt, idx, src, axis=0):
    return tgt.at[idx].add(src)

def _segment_sum(src, seg, n):
    return jax.ops.segment_sum(src, seg, n)
kernel_name = 'mk_prb_d1_jaxref_r2_31404b'

def setup_inputs(seed: int=0):
    np.random.seed(seed)
    _w = jnp.asarray

    def _L0_attn_setup():
        import jax, jax.numpy as jnp
        import numpy as np
        D_MODEL = 1024
        NHEAD = 16
        LN_EPS = 1e-05
        key = jax.random.key(seed)
        ks = jax.random.split(key, 6)
        scale = 1.0 / np.sqrt(D_MODEL)
        return {'x': jax.random.normal(ks[0], (4, 2048, D_MODEL), dtype=jnp.float32), 'Wq': jax.random.normal(ks[1], (D_MODEL, D_MODEL), dtype=jnp.float32) * scale, 'Wv': jax.random.normal(ks[2], (D_MODEL, D_MODEL), dtype=jnp.float32) * scale, 'Wg': jax.random.normal(ks[3], (D_MODEL, D_MODEL), dtype=jnp.float32) * scale, 'Wo': jax.random.normal(ks[4], (D_MODEL, D_MODEL), dtype=jnp.float32) * scale, 'beta': jnp.full((NHEAD,), -0.2, dtype=jnp.float32), 'ln_g': jnp.ones((D_MODEL,), dtype=jnp.float32), 'ln_b': jnp.zeros((D_MODEL,), dtype=jnp.float32)}
    _L0_attn_in = _L0_attn_setup()

    def _L0_ffn_setup():
        import jax, jax.numpy as jnp
        import numpy as np
        B, S, D = (1, 512, 1024)
        E, K, F = (64, 8, 384)
        C = 128

        def _moe(x, router_w, w1, v1, w2):
            T = x.shape[0]
            logits = x @ router_w.T
            probs = jax.nn.softmax(logits, axis=-1)
            wts, idx = jax.lax.top_k(probs, K)
            wts = wts / jnp.sum(wts, axis=-1, keepdims=True)
            R = T * K
            e_flat = idx.reshape(-1)
            tok = jnp.arange(R) // K
            order = jnp.argsort(e_flat)
            e_s, tok_s = (e_flat[order], tok[order])
            w_s = wts.reshape(-1)[order]
            counts = jnp.bincount(e_flat, length=E)
            starts = jnp.cumsum(counts) - counts
            pos = jnp.arange(R) - starts[e_s]
            valid = pos < C
            pos_c = jnp.minimum(pos, C - 1)
            xg = jnp.zeros((E, C, D), x.dtype).at[e_s, pos_c].add(jnp.where(valid[:, None], x[tok_s], 0.0))
            h = jax.nn.silu(jnp.einsum('ecd,efd->ecf', xg, w1)) * jnp.einsum('ecd,efd->ecf', xg, v1)
            y = jnp.einsum('ecf,efd->ecd', h, w2)
            yr = y[e_s, pos_c] * jnp.where(valid, w_s, 0.0)[:, None]
            return jnp.zeros((T, D), x.dtype).at[tok_s].add(yr)
        key = jax.random.key(seed)
        k0, k1, k2, k3, k4 = jax.random.split(key, 5)
        return {'hidden_states': jax.random.normal(k0, (B, S, D), jnp.float32), 'router_w': jax.random.normal(k1, (E, D), jnp.float32) * 0.02, 'w1': jax.random.normal(k2, (E, F, D), jnp.float32) * 0.02, 'v1': jax.random.normal(k3, (E, F, D), jnp.float32) * 0.02, 'w2': jax.random.normal(k4, (E, F, D), jnp.float32) * 0.02}
    _L0_ffn_in = _L0_ffn_setup()
    _d = {'L0_attn_x': _L0_attn_in['x'], 'L0_attn_Wq': _L0_attn_in['Wq'], 'L0_attn_Wv': _L0_attn_in['Wv'], 'L0_attn_Wg': _L0_attn_in['Wg'], 'L0_attn_Wo': _L0_attn_in['Wo'], 'L0_attn_beta': _L0_attn_in['beta'], 'L0_attn_ln_g': _L0_attn_in['ln_g'], 'L0_attn_ln_b': _L0_attn_in['ln_b'], 'L0_ffn_router_w': _L0_ffn_in['router_w'], 'L0_ffn_w1': _L0_ffn_in['w1'], 'L0_ffn_v1': _L0_ffn_in['v1'], 'L0_ffn_w2': _L0_ffn_in['w2']}
    _x0 = _d['L0_attn_x']
    _d['L0_attn_x'] = jax.random.normal(jax.random.fold_in(jax.random.key(seed), 1), (4, 1024, 1024), dtype=_x0.dtype)
    del _x0
    return _d

def reference(L0_attn_x, L0_attn_Wq, L0_attn_Wv, L0_attn_Wg, L0_attn_Wo, L0_attn_beta, L0_attn_ln_g, L0_attn_ln_b, L0_ffn_router_w, L0_ffn_w1, L0_ffn_v1, L0_ffn_w2):

    def _L0_attn_ref(x, Wq, Wv, Wg, Wo, beta, ln_g, ln_b):
        import jax, jax.numpy as jnp
        import numpy as np
        D_MODEL = 1024
        NHEAD = 16
        LN_EPS = 1e-05
        B, S, D = x.shape
        H = NHEAD
        Dh = D // H
        q = (x @ Wq).reshape(B, S, H, Dh)
        v = (x @ Wv).reshape(B, S, H, Dh)
        lam = jax.nn.sigmoid(beta)[None, :, None]
        v_t = jnp.moveaxis(v, 1, 0)

        def step(prev, vt):
            new = lam * prev + vt
            return (new, new)
        _, rest = jax.lax.scan(step, v_t[0], v_t[1:])
        states = jnp.concatenate([v_t[:1], rest], axis=0)
        states = jnp.moveaxis(states, 0, 1)
        y = (q * states).reshape(B, S, D)
        mu = jnp.mean(y, axis=-1, keepdims=True)
        var = jnp.var(y, axis=-1, keepdims=True)
        y = (y - mu) * jax.lax.rsqrt(var + LN_EPS) * ln_g + ln_b
        gate = jax.nn.silu(x @ Wg)
        y = y * gate
        return y @ Wo

    def _L0_ffn_ref(hidden_states, router_w, w1, v1, w2):
        import jax, jax.numpy as jnp
        import numpy as np
        B, S, D = (1, 512, 1024)
        E, K, F = (64, 8, 384)
        C = 128

        def _moe(x, router_w, w1, v1, w2):
            T = x.shape[0]
            logits = x @ router_w.T
            probs = jax.nn.softmax(logits, axis=-1)
            wts, idx = jax.lax.top_k(probs, K)
            wts = wts / jnp.sum(wts, axis=-1, keepdims=True)
            R = T * K
            e_flat = idx.reshape(-1)
            tok = jnp.arange(R) // K
            order = jnp.argsort(e_flat)
            e_s, tok_s = (e_flat[order], tok[order])
            w_s = wts.reshape(-1)[order]
            counts = jnp.bincount(e_flat, length=E)
            starts = jnp.cumsum(counts) - counts
            pos = jnp.arange(R) - starts[e_s]
            valid = pos < C
            pos_c = jnp.minimum(pos, C - 1)
            xg = jnp.zeros((E, C, D), x.dtype).at[e_s, pos_c].add(jnp.where(valid[:, None], x[tok_s], 0.0))
            h = jax.nn.silu(jnp.einsum('ecd,efd->ecf', xg, w1)) * jnp.einsum('ecd,efd->ecf', xg, v1)
            y = jnp.einsum('ecf,efd->ecd', h, w2)
            yr = y[e_s, pos_c] * jnp.where(valid, w_s, 0.0)[:, None]
            return jnp.zeros((T, D), x.dtype).at[tok_s].add(yr)
        b, s, d = hidden_states.shape
        x = hidden_states.transpose(1, 0, 2).reshape(s * b, d)
        out = _moe(x, router_w, w1, v1, w2)
        return out.reshape(s, b, d).transpose(1, 0, 2)
    x = L0_attn_x
    xn = _layernorm(x, axis=-1)
    x = x + _L0_attn_ref(xn, L0_attn_Wq, L0_attn_Wv, L0_attn_Wg, L0_attn_Wo, L0_attn_beta, L0_attn_ln_g, L0_attn_ln_b) + _L0_ffn_ref(xn, L0_ffn_router_w, L0_ffn_w1, L0_ffn_v1, L0_ffn_w2)
    return x

_drawn_inputs = setup_inputs


def setup_inputs(seed=0):
    import zlib

    import numpy as np

    out = dict(_drawn_inputs(seed))
    spreads = {'L0_attn_beta': (-0.20000000298023224, 0.6),
     'L0_attn_ln_g': (1.0, 0.2),
     'L0_attn_ln_b': (0.0, 0.1)}
    factors = {'L0_ffn_router_w': 3.898, 'L0_ffn_w1': 3.554, 'L0_ffn_v1': 3.427, 'L0_ffn_w2': 3.444}
    for name, (base, spread) in spreads.items():
        noise = np.random.default_rng([zlib.crc32(name.encode()), seed]).standard_normal(out[name].shape)
        drawn = base * np.exp(spread * noise) if base else spread * noise
        out[name] = jnp.asarray(drawn.astype(out[name].dtype))
    for name, factor in factors.items():
        out[name] = (out[name] * factor).astype(out[name].dtype)
    return out
```

```python
from contextlib import ExitStack

import numpy as np
import concourse.bass as bass
from concourse import mybir

F32 = mybir.dt.float32
F32R = mybir.dt.float32r
I32 = mybir.dt.int32
ALU = mybir.AluOpType
ACT = mybir.ActivationFunctionType
AX_X = mybir.AxisListType.X

P = 128
TB = 512
NT = TB // P
SLOTS = 128
TOPK = 8
SEL = 64
EPB = 9
PIECES = 6
NEG = -3.0e38
EPS = 1e-5


def build(nc, x, proj_w, ew, router, lam_in, g_in, b_in, out, batches, seq, experts):
    D = x.shape[1]
    KC = D // P
    FF = ew.shape[3] * 4 // (KC * 2)
    FC = FF // P
    NTOK = batches * seq
    NB = NTOK // TB
    assert seq == 2 * TB and KC == 8 and experts == (NB - 1) * EPB + 1 and experts <= SEL
    PW = ew.shape[3]
    PK = KC // 4
    assert PW == PK * 2 * FF == FC * (D // 2)
    XW = D + SEL
    HT = 2 * TB * batches
    NPJ = 4 * KC
    RN = 1.0 / D

    ctx = ExitStack()
    with ctx:
        sem_of = {}

        def sem(name):
            sem_of[name] = ctx.enter_context(nc.semaphore(name))
            return sem_of[name]

        top = [0]
        slab_bytes = 203 * 1024
        slab = ctx.enter_context(nc.sbuf_tensor("slab", [P, slab_bytes // 4], F32))
        slab_at = nc.sbuf_base - slab_bytes

        def place(name, shape, dt, at=None):
            size = int(np.prod(shape[1:])) * 4
            if at is None:
                at = top[0]
                top[0] += size
            assert at + size <= slab_bytes, (name, at, size)
            t = nc.alloc_sbuf_tensor_at(name, shape, dt, offset=slab_at + at, align_bytes=4)
            return t

        ident = place("ident", [P, P], F32)
        ones = place("ones", [P, P], F32)
        lam = place("lam", [P, KC], F32)
        ln_g = place("ln_g", [P, KC], F32)
        ln_b = place("ln_b", [P, KC], F32)
        keep = place("keep", [P, NB], F32)
        carry = place("carry", [P, KC], F32)
        start = place("start", [P, KC], F32)
        idx = place("idx", [P, SEL], I32)
        g_idx = place("g_idx", [P, 1], I32)
        s_idx = place("s_idx", [P, 1], I32)
        w_tab = place("w_tab", [P, SEL], F32)
        col = place("col", [P, 8, NT], F32)
        half = place("half", [P, 4], F32)
        xT_hi = place("xT_hi", [P, KC, TB], F32R)
        xT_lo = place("xT_lo", [P, KC, TB], F32R)
        at_y = top[0]
        yb = place("yb", [P, KC, TB], F32)
        z_lo = place("z_lo", [P, KC, TB], F32R, at_y)
        at_g = top[0]
        gb = place("gb", [P, KC, TB], F32)
        z_hi = place("z_hi", [P, KC, TB], F32R, at_g)
        pw_raw = place("pw_raw", [P, 2, KC, P], F32)
        pw_hi = place("pw_hi", [P, 2, KC, P], F32R)
        pw_lo = place("pw_lo", [P, 2, KC, P], F32R)
        st = place("st", [P, TB], F32)
        sq = place("sq", [P, TB], F32)
        y_sum = place("y_sum", [P, TB], F32)
        q_sum = place("q_sum", [P, TB], F32)
        dg_mu = place("dg_mu", [P, NT, P], F32)
        dg_rs = place("dg_rs", [P, NT, P], F32)
        xn = place("xn", [P, D], F32)
        oT = place("oT", [P, TB], F32)
        ot = place("ot", [P, NT, 2 * P], F32)
        at_e = top[0]
        ew_raw = place("ew_raw", [P, 3, PW], F32)
        ew_hi = place("ew_hi", [P, 3, PW], F32R)
        ew_lo = place("ew_lo", [P, 3, PW], F32R)
        xg = place("xg", [P, XW], F32)
        gT_hi = place("gT_hi", [P, KC, P], F32R)
        gT_lo = place("gT_lo", [P, KC, P], F32R)
        sh = place("sh", [P, FF], F32)
        hh = place("hh", [P, FF], F32)
        hT_hi = place("hT_hi", [P, FC, P], F32R)
        hT_lo = place("hT_lo", [P, FC, P], F32R)
        ys = place("ys", [P, D], F32)
        end_e = top[0]
        top[0] = at_e
        xt = place("xt", [P, 8, D], F32)
        keys = place("keys", [P, HT // 2], F32)
        key_base = place("key_base", [P, HT // 2], F32)
        key_iota = place("key_iota", [P, HT // 2], I32, top[0] - HT * 4)
        r_raw = place("r_raw", [P, KC, SEL], F32)
        r_hi = place("r_hi", [P, KC, P], F32R)
        r_lo = place("r_lo", [P, KC, P], F32R)
        lgT = place("lgT", [SEL, TB], F32)
        lg = place("lg", [P, NT, SEL], F32)
        shf = place("shf", [P, NT, SEL], F32)
        ex = place("ex", [P, NT, SEL], F32)
        rep = place("rep", [P, NT, SEL], F32)
        mk = place("mk", [P, NT, 2 * SEL], F32)
        wt = place("wt", [P, 2, NT, SEL], F32)
        m8 = place("m8", [P, NT, 8], F32)
        bn = place("bn", [P, 2, NT, 2, 6], F32)
        mv = place("mv", [P, 2, NT, 2], F32)
        ve = place("ve", [P, NT], F32)
        rs = place("rs", [P, NT], F32)
        sm = place("sm", [P, 2, NT], F32)
        top8 = place("top8", [P, 8], F32)
        l1 = place("l1", [P, SLOTS], F32)
        l2 = place("l2", [SEL, 2 * SLOTS], F32)
        lf = place("lf", [SEL, SLOTS], F32)
        ka = place("ka", [P, SEL], I32)
        kb = place("kb", [P, SEL], I32)
        kc = place("kc", [P, SEL], I32)
        assert top[0] <= end_e, (top[0], end_e)

        psX = ctx.enter_context(nc.psum_tensor("psX", [P, 2, TB], F32))
        psH = ctx.enter_context(nc.psum_tensor("psH", [P, 2, TB], F32))
        psY = ctx.enter_context(nc.psum_tensor("psY", [P, 2, TB], F32))
        psA = ctx.enter_context(nc.psum_tensor("psA", [P, 2, TB], F32))
        chunks = lambda ps: ps[:, :, :].rearrange("p a (b c) -> p (a b) c", c=P)

        scratch = nc.dram_tensor("xn_scratch", (NTOK, XW), F32).ap()

        s_par = sem("s_par")
        s_const = sem("s_const")
        s_vconst = sem("s_vconst")
        s_lam = sem("s_lam")
        s_rhi, s_rlo = sem("s_rhi"), sem("s_rlo")
        s_xld = [sem(f"s_xld{u}") for u in range(8)]
        s_xst = [sem(f"s_xst{u}") for u in range(8)]
        s_wst = sem("s_wst")
        s_wtf = sem("s_wtf")
        s_x0 = sem("s_x0")
        s_bn = sem("s_bn")
        s_rs = sem("s_rs")
        s_xn = sem("s_xn")
        s_pT = sem("s_pT")
        s_phi, s_plo = sem("s_phi"), sem("s_plo")
        s_rt = sem("s_rt")
        s_lgT = sem("s_lgT")
        s_lt = sem("s_lt")
        s_shf = sem("s_shf")
        s_ex = sem("s_ex")
        s_tk = sem("s_tk")
        s_mk = sem("s_mk")
        s_wm = sem("s_wm")
        s_mT = sem("s_mT")
        s_key = sem("s_key")
        s_ext = sem("s_ext")
        s_l1 = sem("s_l1")
        s_l2 = sem("s_l2")
        s_mrg = sem("s_mrg")
        s_lf = sem("s_lf")
        s_lfT = sem("s_lfT")
        s_ix = sem("s_ix")
        s_pw = [sem(f"s_pw{u}") for u in range(2)]
        s_pwhi, s_pwlo = sem("s_pwhi"), sem("s_pwlo")
        s_pj = sem("s_pj")
        s_vq = sem("s_vq")
        s_go = sem("s_go")
        s_car = sem("s_car")
        s_st0 = sem("s_st0")
        s_sq = sem("s_sq")
        s_sum0 = sem("s_sum0")
        s_sum = sem("s_sum")
        s_smm = sem("s_smm")
        s_col = sem("s_col")
        s_rsy = sem("s_rsy")
        s_dg = sem("s_dg")
        s_bc = sem("s_bc")
        s_z = sem("s_z")
        s_zhi, s_zlo = sem("s_zhi"), sem("s_zlo")
        s_oT = sem("s_oT")
        s_oTT = sem("s_oTT")
        s_ot = sem("s_ot")
        s_acc = sem("s_acc")
        s_otf = sem("s_otf")
        s_xnl = sem("s_xnl")
        s_xT = sem("s_xT")
        s_xhi, s_xlo = sem("s_xhi"), sem("s_xlo")
        s_ew = [sem(f"s_ew{u}") for u in range(3)]
        s_ewhi, s_ewlo = sem("s_ewhi"), sem("s_ewlo")
        s_ewu = sem("s_ewu")
        s_gi = sem("s_gi")
        s_g = sem("s_g")
        s_w = sem("s_w")
        s_gT = sem("s_gT")
        s_ghi, s_glo = sem("s_ghi"), sem("s_glo")
        s_si = sem("s_si")
        s_hh = sem("s_hh")
        s_hT = sem("s_hT")
        s_hhi, s_hlo = sem("s_hhi"), sem("s_hlo")
        s_ys = sem("s_ys")
        s_sci = sem("s_sci")
        s_sc = sem("s_sc")
        s_ysf = sem("s_ysf")

        s_passed = sem("s_passed")

        N_PAR = 4
        TKS = 7

        def n1(j, mm, a):
            return NPJ * j + 6 * mm + a

        def half1(j, mm, a):
            return (NPJ // 2) * j + 3 * mm + a // 2

        def n2(j, mm, w):
            return NPJ * j + 3 * KC + 2 * mm + w

        def half2(j, mm):
            return (NPJ // 2) * j + 3 * KC // 2 + mm

        def phases(eng, block):
            block(0, None, False)
            with eng.Fori(1, NB - 1) as j:
                block(j, EPB * (j - 1), False)
            block(NB - 1, EPB * (NB - 2), True)

        def each_qvg(eng, body):
            with eng.Fori(0, KC // 2) as mm:
                body(mm)

        def each_out(eng, last, body):
            if last:
                with eng.Fori(0, KC // 2 - 2) as mm:
                    body(mm, True, True)
                body(KC // 2 - 2, False, True)
                body(KC // 2 - 1, False, False)
            else:
                with eng.Fori(0, KC // 2) as mm:
                    body(mm, True, True)

        def row_of(pp, h, s):
            return (NB - 1 - h) * TB + s * P - pp * (2 * TB)

        def wait_alone(eng, semaphore, value):
            eng.wait_ge(semaphore, value)
            eng.sem_inc(s_passed, 1)

        block = ctx.enter_context(nc.Block())

        @block.sync
        def _(sp):
            sp.sem_inc(s_xT, 1)
            sp.sem_inc(s_wtf, 2)
            sp.dma_start(lam[:, :], lam_in).then_inc(s_par, 16)
            sp.dma_start(ln_g[:, :], g_in).then_inc(s_par, 16)
            sp.dma_start(ln_b[:, :], b_in).then_inc(s_par, 16)
            sp.dma_start(r_raw[:, :, :], router).then_inc(s_par, 16)

            def load_x(row, u):
                sp.dma_start(xt[:, u, :], x[bass.ds(row, P), :]).then_inc(s_xld[u], 16)

            for u in range(8):
                load_x(row_of(0, u // NT, u % NT), u)

            def router_pair(pp, more):
                def store(h):
                    for s in range(NT):
                        u = NT * h + s
                        wait_alone(sp, s_xn, 8 * pp + u + 1)
                        sp.dma_start(scratch[bass.ds(row_of(pp, h, s), P), 0:D],
                                     xt[:, u, :]).then_inc(s_xst[u], 16)

                def reload(h):
                    for s in range(NT):
                        u = NT * h + s
                        sp.wait_ge(s_xst[u], 16 * (pp + 1))
                        wait_alone(sp, s_pT, 8 * pp + u + 1)
                        load_x(row_of(pp + 1, h, s), u)

                def store_w(h):
                    wait_alone(sp, s_wm, 2 * pp + h + 1)
                    for s in range(NT):
                        sp.dma_start(scratch[bass.ds(row_of(pp, h, s), P), D:XW],
                                     wt[:, h, s, :]).then_inc(s_wst, 16)
                    sp.wait_ge(s_wst, 16 * NT * (2 * pp + h + 1))
                    sp.sem_inc(s_wtf, 1)

                store(0)
                store(1)
                if more:
                    reload(0)
                store_w(0)
                if more:
                    reload(1)
                store_w(1)

            def load_proj(slot, row, n_prev=None):
                if n_prev is not None:
                    sp.wait_ge(s_pwlo, n_prev)
                sp.dma_start(pw_raw[:, slot, :, :].rearrange("p k c -> p (k c)"),
                             proj_w[row, :, :]).then_inc(s_pw[slot], 16)

            def load_piece(e, c, n_prev=None):
                if n_prev is not None:
                    sp.wait_ge(s_ewlo, n_prev)
                sp.dma_start(ew_raw[:, c % 3, :], ew[e, c, :, :]).then_inc(s_ew[c % 3], 16)

            def pieces(e, nxt, first):
                for c in range(3):
                    if first and nxt:
                        load_piece(e + 1, c, PIECES * e + 3 + c + 1)
                    if not first:
                        load_piece(e + 1, 3 + c, PIECES * (e + 1) + c + 1)

            with sp.Fori(0, NB // 2 - 1) as pp:
                router_pair(pp, True)
            router_pair(NB // 2 - 1, False)
            for u in range(8):
                sp.wait_ge(s_xst[u], 16 * (NB // 2))
            load_proj(0, 0)
            load_proj(1, 1)
            for b in range(NB):
                sp.dma_start(out[b * TB:(b + 1) * TB, :], x[b * TB:(b + 1) * TB, :]).then_inc(s_x0, 16)
            load_proj(0, 2, 1)
            load_proj(1, 3, 2)

            def run(j, e0, last):
                with_e = e0 is not None

                def qvg(mm):
                    e = None if not with_e else e0 + mm
                    if with_e:
                        load_piece(e + 1, 0, PIECES * e + 4)
                        load_piece(e + 1, 1, PIECES * e + 5)
                        load_piece(e + 1, 2, PIECES * e + 6)
                        load_piece(e + 1, 3, PIECES * e + 7)
                    for a in range(2, 6):
                        load_proj(a % 2, 6 * mm + a + 2, n1(j, mm, a) + 1)
                    if with_e:
                        load_piece(e + 1, 4, PIECES * e + 8)
                        load_piece(e + 1, 5, PIECES * e + 9)
                    for a in range(6, 8):
                        load_proj(a % 2, 6 * mm + a + 2, n1(j, mm, a) + 1)

                each_qvg(sp, qvg)
                if with_e:
                    pieces(e0 + 4, True, True)
                    pieces(e0 + 4, True, False)
                else:
                    sp.wait_ge(s_l1, SLOTS // 8)
                    sp.dma_start(l2[:, SLOTS:2 * SLOTS], l1[SEL:2 * SEL, :]).then_inc(s_l2, 16)

                def outp(mm, loads, splits):
                    if not last:
                        sp.wait_ge(s_xT, 4 * j + mm + 1)
                        sp.dma_start(xn[:, :], scratch[bass.ds((j + 1) * TB + mm * P, P), 0:D]
                                     ).then_inc(s_xnl, 16)
                    if with_e:
                        e = e0 + 5 + mm
                        pieces(e, True, True)
                        pieces(e, True, False)
                    for w in range(2, 4):
                        if loads:
                            load_proj(w % 2, 3 * KC + 2 * mm + w + 2, n2(j, mm, w) + 1)

                each_out(sp, last, outp)
                if not with_e:
                    sp.wait_ge(s_ix, 5)
                    for c in range(3):
                        load_piece(0, c)
                    for c in range(3):
                        load_piece(0, 3 + c, c + 1)

            phases(sp, run)

        @block.gpsimd
        def _(pool):
            pool.sem_inc(s_sum, 1)
            pool.sem_inc(s_otf, 1)
            pool.sem_inc(s_ysf, 1)
            pool.memset(ident[:, :], 0.0).then_inc(s_const, 1)
            for h in range(2):
                pool.wait_ge(s_const, h + 1)
                pool.iota(key_iota[h * SEL:(h + 1) * SEL, :], pattern=[[-1, HT // 2]],
                          base=HT - h * (HT // 2), channel_multiplier=0).then_inc(s_const, 1)
            pool.wait_ge(s_const, 3)
            pool.affine_select(out=ident[:, :], in_=ident[:, :], compare_op=ALU.not_equal, fill=1.0, base=0,
                               pattern=[[-1, P]], channel_multiplier=1).then_inc(s_const, 1)
            pool.wait_ge(s_const, 4)
            pool.tensor_copy(key_base[:, :], key_iota[:, :]).then_inc(s_const, 1)

            pool.wait_ge(s_vconst, 1)
            with pool.Fori(0, NB) as qq:
                pool.wait_ge(s_bn, 3 * qq + 3)
                pool.tensor_tensor(rs[:, :], ve[:, :], half[:, 0:NT], ALU.pow).then_inc(s_rs, 1)

            def gather(e):
                pool.tensor_copy(g_idx[:, :], idx[:, bass.ds(e, 1)]).then_inc(s_gi, 1)
                wait_alone(pool, s_gi, e + 1)
                pool.indirect_dma_start(xg[:, :], None, scratch,
                                        bass.IndirectOffsetOnAxis(ap=g_idx[:, 0:1], axis=0)
                                        ).then_inc(s_g, 16)

            def gather_next(e):
                pool.wait_ge(s_gT, e + 1)
                pool.wait_ge(s_w, e + 1)
                gather(e + 1)

            def scatter(e):
                pool.tensor_copy(s_idx[:, :], idx[:, bass.ds(e, 1)]).then_inc(s_sci, 1)
                pool.wait_ge(s_sci, e + 1)
                wait_alone(pool, s_ys, e + 1)
                pool.indirect_dma_start(out, bass.IndirectOffsetOnAxis(ap=s_idx[:, 0:1], axis=0),
                                        ys[:, :], None, compute_op=ALU.add).then_inc(s_sc, 16)
                pool.wait_ge(s_sc, 16 * (e + 1))
                pool.sem_inc(s_ysf, 1)

            def add_sums(j, mm, h):
                i = KC * j + 2 * mm + h
                pool.wait_ge(s_sq, i + 1)
                pool.wait_ge(s_sum, i + 1)
                pool.tensor_tensor(y_sum[:, :], y_sum[:, :], yb[:, 2 * mm + h, :], ALU.add)
                pool.tensor_tensor(q_sum[:, :], q_sum[:, :], sq[:, :], ALU.add).then_inc(s_sum, 1)

            def run(j, e0, last):
                with_e = e0 is not None
                if with_e:
                    wait_alone(pool, s_smm, j)
                pool.memset(y_sum[:, :], 0.0)
                pool.memset(q_sum[:, :], 0.0).then_inc(s_sum0, 1)
                wait_alone(pool, s_sum0, j + 1)

                def qvg(mm):
                    if with_e:
                        gather_next(e0 + mm)
                    add_sums(j, mm, 0)
                    if with_e:
                        scatter(e0 + mm)
                    add_sums(j, mm, 1)

                each_qvg(pool, qvg)
                if with_e:
                    gather_next(e0 + 4)
                pool.wait_ge(s_col, 4 * j + 4)
                pool.tensor_tensor(col[:, 5, :], col[:, 4, :], half[:, 0:NT], ALU.pow).then_inc(s_rsy, 1)

                def z_lows(m0):
                    with pool.Fori(m0, m0 + KC // 2) as m:
                        pool.wait_ge(s_zhi, KC * j + m + 1)
                        pool.tensor_tensor(z_lo[:, m, :], yb[:, m, :], z_hi[:, m, :].bitcast(F32),
                                           ALU.subtract).then_inc(s_zlo, 1)

                z_lows(0)
                if with_e:
                    scatter(e0 + 4)
                z_lows(KC // 2)
                if not with_e:
                    pool.wait_ge(s_x0, 16 * NB)

                def outp(mm, loads, splits):
                    if with_e:
                        gather_next(e0 + 5 + mm)
                        scatter(e0 + 5 + mm)
                    pool.wait_ge(s_ot, KC * j + 2 * mm + 2)
                    pool.dma_start(out[bass.ds(j * TB, TB), bass.ds(mm * 2 * P, 2 * P)]
                                   .rearrange("(t p) c -> p t c", p=P), ot[:, :, :],
                                   accum_op=ALU.add).then_inc(s_acc, 16)
                    pool.wait_ge(s_acc, 16 * (4 * j + mm + 1))
                    pool.sem_inc(s_otf, 1)

                each_out(pool, last, outp)
                if not with_e:
                    pool.wait_ge(s_ix, 5)
                    pool.wait_ge(s_wst, 16 * NB * NT)
                    for u in range(8):
                        pool.wait_ge(s_xst[u], 16 * (NB // 2))
                    gather(0)

            phases(pool, run)
            scatter(experts - 1)

        @block.scalar
        def _(act):
            act.sem_inc(s_go, 2)
            act.wait_ge(s_par, 16 * N_PAR)
            act.activation(lam[:, :], lam[:, :], ACT.Sigmoid).then_inc(s_lam, 1)
            act.wait_ge(s_vconst, 1)
            act.activation(r_hi[:, :, 0:SEL], r_raw[:, :, :], ACT.Copy).then_inc(s_rhi, 1)

            def router_block(pp, h):
                q = 2 * pp + h
                dst = (z_hi, xT_hi)[h]
                for s in range(NT):
                    act.wait_ge(s_pT, NT * q + s + 1)
                    act.activation(dst[:, :, s * P:(s + 1) * P], chunks((psX, psH)[s % 2]),
                                   ACT.Copy).then_inc(s_phi, 1)
                act.wait_ge(s_rt, q + 1)
                act.activation(lgT[:, :], psA[0:SEL, 0, :], ACT.Copy).then_inc(s_lgT, 1)
                act.wait_ge(s_shf, q + 1)
                act.activation(ex[:, :, :], shf[:, :, :], ACT.Exp).then_inc(s_ex, 1)

            with act.Fori(0, NB // 2) as pp:
                router_block(pp, 0)
                router_block(pp, 1)

            def proj_hi(n, slot, hf, used):
                act.wait_ge(s_pw[slot], 16 * (hf + 1))
                if used is not None:
                    act.wait_ge(s_pj, used)
                act.activation(pw_hi[:, slot, :, :], pw_raw[:, slot, :, :], ACT.Copy).then_inc(s_pwhi, 1)

            def piece_hi(e, c, used=True):
                act.wait_ge(s_ew[c % 3], 16 * (2 * e + c // 3 + 1))
                if used:
                    act.wait_ge(s_ewu, PIECES * e + c - 2)
                act.activation(ew_hi[:, c % 3, :], ew_raw[:, c % 3, :], ACT.Copy).then_inc(s_ewhi, 1)

            def silu_h(e):
                act.wait_ge(s_ewu, PIECES * e + 4)
                act.activation(sh[:, :], psH[:, 0, 0:FF], ACT.Silu).then_inc(s_si, 1)

            def hT_hi_of(e):
                act.wait_ge(s_hT, e + 1)
                act.activation(hT_hi[:, :, :].rearrange("p f c -> p (f c)"), psX[:, 0, 0:FF],
                               ACT.Copy).then_inc(s_hhi, 1)

            def y_out(e):
                act.wait_ge(s_w, e + 1)
                act.wait_ge(s_ysf, e + 1)
                for h in range(2):
                    wait_alone(act, s_ewu, PIECES * e + 5 + h)
                    o = act.activation(ys[:, h * TB:(h + 1) * TB], psY[:, h, :], ACT.Copy,
                                       scale=w_tab[:, bass.ds(e, 1)])
                o.then_inc(s_ys, 1)

            def gT_hi_of(e):
                wait_alone(act, s_g, 16 * (e + 1))
                act.activation(w_tab[:, bass.ds(e, 1)], xg[:, bass.ds(e + D, 1)], ACT.Copy).then_inc(s_w, 1)
                act.wait_ge(s_gT, e + 1)
                act.activation(gT_hi[:, :, :], chunks(psX), ACT.Copy).then_inc(s_ghi, 1)

            def square(j, mm, h):
                act.wait_ge(s_vq, 16 * j + 4 * mm + 2 * h + 3)
                act.wait_ge(s_sum, KC * j + 2 * mm + h + 1)
                act.activation(sq[:, :], yb[:, 2 * mm + h, :], ACT.Square).then_inc(s_sq, 1)

            def gate(j, mm, h):
                act.wait_ge(s_pj, n1(j, mm, 3 * h + 2) + 1)
                act.activation(gb[:, 2 * mm + h, :], psA[:, h, :], ACT.Silu).then_inc(s_go, 1)

            def z_his(j, m0):
                with act.Fori(m0, m0 + KC // 2) as m:
                    act.wait_ge(s_z, 3 * KC * j + 3 * m + 3)
                    act.activation(z_hi[:, m, :], yb[:, m, :], ACT.Copy).then_inc(s_zhi, 1)

            def out_copy(j, mm, w):
                act.wait_ge(s_pj, n2(j, mm, w) + 1)
                act.activation(oT[:, :], psA[:, w, :], ACT.Copy).then_inc(s_go, 1)

            for n in range(2):
                proj_hi(n, n, 0, None)

            def run(j, e0, last):
                with_e = e0 is not None

                def qvg(mm):
                    e = None if not with_e else e0 + mm
                    S = lambda a: proj_hi(None, a % 2, half1(j, mm, a), n1(j, mm, a) - 1)
                    if with_e:
                        for c in (3, 4, 5):
                            piece_hi(e, c)
                        silu_h(e)
                        piece_hi(e + 1, 0)
                    S(2)
                    S(3)
                    if with_e:
                        hT_hi_of(e)
                    square(j, mm, 0)
                    gate(j, mm, 0)
                    S(4)
                    if with_e:
                        y_out(e)
                        piece_hi(e + 1, 1)
                        piece_hi(e + 1, 2)
                        gT_hi_of(e + 1)
                    S(5)
                    S(6)
                    square(j, mm, 1)
                    gate(j, mm, 1)
                    S(7)

                each_qvg(act, qvg)
                if with_e:
                    e = e0 + 4
                    for c in (3, 4, 5):
                        piece_hi(e, c)
                    silu_h(e)
                    hT_hi_of(e)
                z_his(j, 0)
                if with_e:
                    y_out(e)
                    for c in range(3):
                        piece_hi(e + 1, c)
                    gT_hi_of(e + 1)
                z_his(j, KC // 2)

                def outp(mm, loads, splits):
                    if with_e:
                        e = e0 + 5 + mm
                        for c in (3, 4, 5):
                            piece_hi(e, c)
                        silu_h(e)
                        piece_hi(e + 1, 0)
                    out_copy(j, mm, 0)
                    if with_e:
                        hT_hi_of(e)
                    if not last:
                        act.wait_ge(s_xT, 4 * j + mm + 2)
                        act.activation(xT_hi[:, :, bass.ds(mm * P, P)], chunks(psH), ACT.Copy).then_inc(s_xhi, 1)
                    if splits:
                        proj_hi(None, 0, half2(j, mm + 1), n2(j, mm, 2) - 1)
                    if with_e:
                        y_out(e)
                        piece_hi(e + 1, 1)
                        piece_hi(e + 1, 2)
                        gT_hi_of(e + 1)
                    out_copy(j, mm, 1)
                    if splits:
                        proj_hi(None, 1, half2(j, mm + 1), n2(j, mm, 3) - 1)

                each_out(act, last, outp)
                if not with_e:
                    for c in range(3):
                        piece_hi(0, c, used=False)
                    gT_hi_of(0)

            phases(act, run)
            e = experts - 1
            for c in (3, 4, 5):
                piece_hi(e, c)
            silu_h(e)
            hT_hi_of(e)
            y_out(e)

        @block.vector
        def _(dve):
            dve.sem_inc(s_vq, 1)
            dve.memset(r_hi[:, :, :].bitcast(F32), 0.0)
            dve.memset(r_lo[:, :, :].bitcast(F32), 0.0)
            dve.memset(carry[:, :], 0.0).then_inc(s_car, 1)
            dve.memset(idx[:, :], 0)
            dve.memset(ones[:, :], 1.0)
            dve.memset(half[:, :], -0.5)
            dve.memset(wt[:, :, :, :], 0.0)
            for b in range(NB):
                dve.memset(keep[:, b:b + 1], float(b % 2))
            dve.memset(mk[:, :, :], 0.0).then_inc(s_vconst, 1)
            dve.wait_ge(s_vconst, 1)
            dve.wait_ge(s_rhi, 1)
            dve.tensor_tensor(r_lo[:, :, 0:SEL], r_raw[:, :, :], r_hi[:, :, 0:SEL].bitcast(F32),
                              ALU.subtract).then_inc(s_rlo, 1)

            def norm_block(pp, h):
                q = 2 * pp + h
                for s in range(NT):
                    dve.wait_ge(s_xld[NT * h + s], 16 * (pp + 1))
                    for i in range(2):
                        o = dve.bn_stats(bn[:, h, s, i, :], xt[:, NT * h + s, i * TB:(i + 1) * TB])
                o.then_inc(s_bn, 1)
                wait_alone(dve, s_bn, 3 * q + 1)
                for s in range(NT):
                    o = dve.bn_aggr(mv[:, h, s, :], bn[:, h, s, :, :].rearrange("p a b -> p (a b)"))
                o.then_inc(s_bn, 1)
                dve.wait_ge(s_bn, 3 * q + 2)
                dve.tensor_scalar(ve[:, :], mv[:, h, :, 1], EPS, None, ALU.add).then_inc(s_bn, 1)
                dve.wait_ge(s_rs, q + 1)
                for s in range(NT):
                    u = NT * h + s
                    dve.tensor_scalar(xt[:, u, :], xt[:, u, :], mv[:, h, s, 0:1], rs[:, s:s + 1],
                                      ALU.subtract, ALU.mult).then_inc(s_xn, 1)

            def lows(pp, h):
                dst, hi = ((z_lo, z_hi), (xT_lo, xT_hi))[h]
                for s in range(NT):
                    dve.wait_ge(s_phi, NT * (2 * pp + h) + s + 1)
                    c = slice(s * P, (s + 1) * P)
                    dve.tensor_tensor(dst[:, :, c], chunks((psX, psH)[s % 2]), hi[:, :, c].bitcast(F32),
                                      ALU.subtract).then_inc(s_plo, 1)

            def top8_of(pp, h):
                q = 2 * pp + h
                E = experts
                own = lambda i: dve.wait_ge(s_tk, TKS * q + i)
                dve.wait_ge(s_lt, q + 1)
                dve.tensor_copy(lg[:, :, :], psA[:, 1, 0:NT * SEL].rearrange("p (s e) -> p s e", e=SEL)
                                ).then_inc(s_tk, 1)
                wait_alone(dve, s_tk, TKS * q + 1)
                for s in range(NT):
                    o = dve.max(m8[:, s, :], lg[:, s, 0:E])
                o.then_inc(s_tk, 1)
                own(2)
                dve.tensor_tensor(shf[:, :, :], lg[:, :, :], m8[:, :, 0:1].to_broadcast([P, NT, SEL]),
                                  ALU.subtract).then_inc(s_shf, 1)
                for s in range(NT):
                    o = dve.match_replace(rep[:, s, 0:E], m8[:, s, :], lg[:, s, 0:E], NEG)
                o.then_inc(s_tk, 1)
                own(3)
                m = mk[:, :, (1 - h) * SEL:(1 - h) * SEL + E]
                dve.tensor_scalar(m, rep[:, :, 0:E], NEG, None, ALU.is_equal).then_inc(s_tk, 1)
                own(4)
                dve.wait_ge(s_ex, q + 1)
                w = wt[:, h, :, 0:E]
                dve.wait_ge(s_wtf, q + 1)
                dve.tensor_tensor(w, ex[:, :, 0:E], m, ALU.mult).then_inc(s_tk, 1)
                own(5)
                dve.tensor_reduce(sm[:, 0, :], w, AX_X, ALU.add).then_inc(s_tk, 1)
                own(6)
                dve.reciprocal(sm[:, 1, :], sm[:, 0, :]).then_inc(s_tk, 1)
                own(7)
                dve.tensor_tensor(w, w, sm[:, 1, :].unsqueeze(2).to_broadcast([P, NT, E]),
                                  ALU.mult).then_inc(s_wm, 1)

            def keys_of(pp):
                wait_alone(dve, s_mT, pp + 1)
                b = batches - 1 - pp
                view = lambda t: t[:, :].rearrange("p (s b) -> p s b", b=batches)[:, :, bass.ds(b, 1)]
                dve.scalar_tensor_tensor(view(keys), psY[:, 0, :].unsqueeze(2), float(HT), view(key_base),
                                         ALU.mult, ALU.add).then_inc(s_key, 1)

            def pair(pp, more):
                lows(pp, 0)
                norm_block(pp, 1)
                top8_of(pp, 0)
                lows(pp, 1)
                if more:
                    norm_block(pp + 1, 0)
                top8_of(pp, 1)
                keys_of(pp)

            dve.wait_ge(s_const, 5)
            norm_block(0, 0)
            with dve.Fori(0, NB // 2 - 1) as pp:
                pair(pp, True)
            pair(NB // 2 - 1, False)

            def extract(src, into, n, steps, copied):
                dve.max(top8[0:src.shape[0], :], src).then_inc(steps, 1)
                dve.wait_ge(steps, 2 * n + 1)
                dve.tensor_copy(into[:, bass.ds(n * 8, 8)], top8[0:src.shape[0], :]).then_inc(copied, 1)
                dve.match_replace(src, top8[0:src.shape[0], :], src, -1.0).then_inc(steps, 1)
                wait_alone(dve, steps, 2 * n + 2)

            def proj_lo(n, slot):
                dve.wait_ge(s_pwhi, n + 1)
                dve.tensor_tensor(pw_lo[:, slot, :, :], pw_raw[:, slot, :, :], pw_hi[:, slot, :, :].bitcast(F32),
                                  ALU.subtract).then_inc(s_pwlo, 1)

            def piece_lo(e, c):
                dve.wait_ge(s_ewhi, PIECES * e + c + 1)
                dve.tensor_tensor(ew_lo[:, c % 3, :], ew_raw[:, c % 3, :], ew_hi[:, c % 3, :].bitcast(F32),
                                  ALU.subtract).then_inc(s_ewlo, 1)

            def hidden(e):
                dve.wait_ge(s_si, e + 1)
                dve.tensor_tensor(hh[:, :], psH[:, 1, 0:FF], sh[:, :], ALU.mult).then_inc(s_hh, 1)

            def hT_lo_of(e):
                dve.wait_ge(s_hhi, e + 1)
                dve.tensor_tensor(hT_lo[:, :, :].rearrange("p f c -> p (f c)"), psX[:, 0, 0:FF],
                                  hT_hi[:, :, :].rearrange("p f c -> p (f c)").bitcast(F32),
                                  ALU.subtract).then_inc(s_hlo, 1)

            def gT_lo_of(e):
                dve.wait_ge(s_ghi, e + 1)
                dve.tensor_tensor(gT_lo[:, :, :], chunks(psX), gT_hi[:, :, :].bitcast(F32),
                                  ALU.subtract).then_inc(s_glo, 1)

            def scan(j, mm, h):
                m = 2 * mm + h
                dve.wait_ge(s_pj, n1(j, mm, 3 * h) + 1)
                dve.tensor_tensor_scan(st[:, :], lam[:, bass.ds(m, 1)].to_broadcast([P, TB]), psA[:, h, :],
                                       start[:, bass.ds(m, 1)], ALU.mult, ALU.add).then_inc(s_vq, 1)

            def times_q(j, mm, h):
                m = 2 * mm + h
                dve.wait_ge(s_pj, n1(j, mm, 3 * h + 1) + 1)
                dve.wait_ge(s_vq, 16 * j + 4 * mm + 2 * h + 2)
                dve.tensor_tensor(yb[:, m, :], psA[:, 1 - h, :], st[:, :], ALU.mult).then_inc(s_vq, 1)
                dve.tensor_copy(carry[:, bass.ds(m, 1)], st[:, TB - 1:TB]).then_inc(s_car, 1)

            def z_of(j, m0):
                with dve.Fori(m0, m0 + KC // 2) as m:
                    own = lambda i: dve.wait_ge(s_z, 3 * KC * j + 3 * m + i)
                    dve.tensor_tensor(yb[:, m, :], yb[:, m, :], psA[:, 0, :], ALU.subtract).then_inc(s_z, 1)
                    own(1)
                    dve.scalar_tensor_tensor(yb[:, m, :], yb[:, m, :], ln_g[:, bass.ds(m, 1)], psA[:, 1, :],
                                             ALU.mult, ALU.mult).then_inc(s_z, 1)
                    own(2)
                    dve.scalar_tensor_tensor(yb[:, m, :], yb[:, m, :], ln_b[:, bass.ds(m, 1)], gb[:, m, :],
                                             ALU.add, ALU.mult).then_inc(s_z, 1)

            def token_stats(j):
                own = lambda i: dve.wait_ge(s_col, 4 * j + i)
                dve.wait_ge(s_smm, j + 1)
                dve.tensor_scalar(col[:, 0:2, :], psA[:, 0, 0:2 * NT].rearrange("p (i t) -> p i t", t=NT),
                                  RN, None, ALU.mult).then_inc(s_col, 1)
                own(1)
                dve.tensor_tensor(col[:, 2, :], col[:, 0, :], col[:, 0, :], ALU.mult).then_inc(s_col, 1)
                own(2)
                dve.tensor_tensor(col[:, 3, :], col[:, 1, :], col[:, 2, :], ALU.subtract).then_inc(s_col, 1)
                own(3)
                dve.tensor_scalar(col[:, 4, :], col[:, 3, :], 0.0, EPS, ALU.max, ALU.add).then_inc(s_col, 1)
                eye = ident[:, :].unsqueeze(1).to_broadcast([P, NT, P])
                dve.tensor_tensor(dg_mu[:, :, :], eye, col[:, 0, :].unsqueeze(2).to_broadcast([P, NT, P]),
                                  ALU.mult)
                dve.wait_ge(s_rsy, j + 1)
                dve.tensor_tensor(dg_rs[:, :, :], eye, col[:, 5, :].unsqueeze(2).to_broadcast([P, NT, P]),
                                  ALU.mult).then_inc(s_dg, 1)
                dve.wait_ge(s_bc, j + 1)
                wait_alone(dve, s_go, 16 * j + 8 + 2)

            def out_rows(j, mm, w):
                i = KC * j + 2 * mm + w
                dve.wait_ge(s_oTT, i + 1)
                if w == 0:
                    dve.wait_ge(s_otf, 4 * j + mm + 1)
                src = (psX[:, 1, :], psY[:, 0, :])[w].rearrange("p (t c) -> p t c", c=P)
                dve.tensor_copy(ot[:, :, w * P:(w + 1) * P], src).then_inc(s_ot, 1)

            for n in range(2):
                proj_lo(n, n)

            def run(j, e0, last):
                with_e = e0 is not None
                dve.wait_ge(s_car, KC * j + 1)
                dve.tensor_scalar(start[:, :], carry[:, :], keep[:, bass.ds(j, 1)], None,
                                  ALU.mult).then_inc(s_st0, 1)
                wait_alone(dve, s_st0, j + 1)
                if not with_e:
                    dve.wait_ge(s_key, NB // 2)
                    dve.wait_ge(s_lam, 1)

                def qvg(mm):
                    e = None if not with_e else e0 + mm
                    S = lambda a: proj_lo(n1(j, mm, a), a % 2)

                    def round_(r):
                        if not with_e:
                            extract(keys[:, :], l1, 4 * mm + r, s_ext, s_l1)

                    if with_e:
                        for c in (3, 4, 5):
                            piece_lo(e, c)
                        hidden(e)
                        piece_lo(e + 1, 0)
                    round_(0)
                    scan(j, mm, 0)
                    S(2)
                    round_(1)
                    times_q(j, mm, 0)
                    S(3)
                    if with_e:
                        hT_lo_of(e)
                    round_(2)
                    S(4)
                    if with_e:
                        piece_lo(e + 1, 1)
                        piece_lo(e + 1, 2)
                        gT_lo_of(e + 1)
                    round_(3)
                    scan(j, mm, 1)
                    S(5)
                    times_q(j, mm, 1)
                    S(6)
                    S(7)

                each_qvg(dve, qvg)
                if with_e:
                    e = e0 + 4
                    for c in (3, 4, 5):
                        piece_lo(e, c)
                    hidden(e)
                else:
                    dve.wait_ge(s_l1, SLOTS // 8)
                    dve.tensor_copy(l2[:, 0:SLOTS], l1[0:SEL, :]).then_inc(s_lf, 1)
                token_stats(j)
                if with_e:
                    hT_lo_of(e)
                z_of(j, 0)
                if with_e:
                    for c in range(3):
                        piece_lo(e + 1, c)
                    gT_lo_of(e + 1)
                z_of(j, KC // 2)
                if not with_e:
                    dve.wait_ge(s_l2, 16)
                    dve.wait_ge(s_lf, 1)

                def outp(mm, loads, splits):
                    if with_e:
                        e = e0 + 5 + mm
                        for c in (3, 4, 5):
                            piece_lo(e, c)
                        hidden(e)
                        piece_lo(e + 1, 0)
                        hT_lo_of(e)
                    else:
                        for r in range(4):
                            extract(l2[:, :], lf, 4 * mm + r, s_mrg, s_lf)
                    out_rows(j, mm, 0)
                    if not last:
                        dve.wait_ge(s_xhi, 4 * j + mm + 1)
                        c = bass.ds(mm * P, P)
                        dve.tensor_tensor(xT_lo[:, :, c], chunks(psH), xT_hi[:, :, c].bitcast(F32),
                                          ALU.subtract).then_inc(s_xlo, 1)
                    if splits:
                        proj_lo(n2(j, mm, 2), 0)
                    if with_e:
                        piece_lo(e + 1, 1)
                        piece_lo(e + 1, 2)
                        gT_lo_of(e + 1)
                    out_rows(j, mm, 1)
                    if splits:
                        proj_lo(n2(j, mm, 3), 1)

                each_out(dve, last, outp)
                if not with_e:
                    own = lambda i: dve.wait_ge(s_ix, i)
                    dve.wait_ge(s_lfT, 1)
                    dve.tensor_scalar(ka[:, :], psX[:, 0, 0:SEL], -1.0, float(2 * HT), ALU.mult,
                                      ALU.add).then_inc(s_ix, 1)
                    own(1)
                    dve.tensor_scalar(kb[:, :], ka[:, :], batches - 1, seq.bit_length() - 1, ALU.bitwise_and,
                                      ALU.logical_shift_left).then_inc(s_ix, 1)
                    own(2)
                    dve.tensor_scalar(kc[:, :], ka[:, :], HT - 1, batches.bit_length() - 1, ALU.bitwise_and,
                                      ALU.logical_shift_right).then_inc(s_ix, 1)
                    own(3)
                    dve.tensor_tensor(idx[:, 0:experts], kb[:, 0:experts], kc[:, 0:experts],
                                      ALU.add).then_inc(s_ix, 2)
                    for c in range(3):
                        piece_lo(0, c)
                    gT_lo_of(0)

            phases(dve, run)
            e = experts - 1
            for c in (3, 4, 5):
                piece_lo(e, c)
            hidden(e)
            hT_lo_of(e)

        @block.tensor
        def _(pe):
            def three(dst, l_hi, l_lo, r_hi_, r_lo_, first, last):
                pe.matmul(dst, l_hi, r_hi_, start=first, stop=False)
                pe.matmul(dst, l_hi, r_lo_, start=False, stop=False)
                return pe.matmul(dst, l_lo, r_hi_, start=False, stop=last)

            pe.wait_ge(s_const, 5)
            pe.wait_ge(s_vconst, 1)
            pe.wait_ge(s_rlo, 1)

            def router_block(pp, h):
                q = 2 * pp + h
                hi, lo = ((z_hi, z_lo), (xT_hi, xT_lo))[h]
                for s in range(NT):
                    pe.wait_ge(s_xn, NT * q + s + 1)
                    if s >= 2:
                        pe.wait_ge(s_plo, NT * q + s - 1)
                    bank = (psX, psH)[s % 2]
                    for k in range(KC):
                        o = pe.transpose(bank[:, k // 4, (k % 4) * P:(k % 4 + 1) * P],
                                         xt[:, NT * h + s, k * P:(k + 1) * P], ident[:, :])
                    o.then_inc(s_pT, 1)
                pe.wait_ge(s_plo, NT * q + NT)
                for k in range(KC):
                    three(psA[:, 0, :], r_hi[:, k, :], r_lo[:, k, :], hi[:, k, :], lo[:, k, :], k == 0, False)
                    o = pe.matmul(psA[:, 0, :], r_lo[:, k, :], lo[:, k, :], start=False, stop=k == KC - 1)
                o.then_inc(s_rt, 1)
                wait_alone(pe, s_lgT, q + 1)
                for s in range(NT):
                    o = pe.transpose(psA[:, 1, s * SEL:(s + 1) * SEL], lgT[:, s * P:(s + 1) * P],
                                     ident[0:SEL, 0:SEL])
                o.then_inc(s_lt, 1)

            with pe.Fori(0, NB // 2) as pp:
                router_block(pp, 0)
                router_block(pp, 1)
                pe.wait_ge(s_tk, TKS * (2 * pp + 1) + 4)
                for s in range(NT):
                    o = pe.transpose(psY[:, 0, s * P:(s + 1) * P], mk[:, s, :], ident[:, :])
                o.then_inc(s_mT, 1)

            def proj(n, bank, slot, hi, lo):
                pe.wait_ge(s_pwlo, n + 1)
                for k in range(KC):
                    o = three(psA[:, bank, :], pw_hi[:, slot, k, :], pw_lo[:, slot, k, :], hi[:, k, :],
                              lo[:, k, :], k == 0, k == KC - 1)
                o.then_inc(s_pj, 1)

            def qvg_proj(j, mm, a):
                vq = {0: 0, 2: 1, 3: 2, 5: 3}
                go = {0: -1, 1: 0, 4: 1}
                if a in vq:
                    pe.wait_ge(s_vq, 16 * j + 4 * mm + vq[a] + 1)
                if a in go:
                    pe.wait_ge(s_go, 16 * j + 2 * mm + go[a] + 2)
                proj(n1(j, mm, a), a % 2, a % 2, xT_hi, xT_lo)

            def out_proj(j, mm, w):
                if w == 0:
                    pe.wait_ge(s_vq, 16 * j + 16 + 1)
                    pe.wait_ge(s_go, 16 * j + 7 + 2 * mm + 2)
                    pe.wait_ge(s_zlo, KC * (j + 1))
                else:
                    pe.wait_ge(s_go, 16 * j + 8 + 2 * mm + 2)
                proj(n2(j, mm, w), w, w, z_hi, z_lo)

            def out_turn(j, mm, w):
                pe.wait_ge(s_go, 16 * j + 8 + 2 * mm + w + 1 + 2)
                dst = (psX[:, 1, :], psY[:, 0, :])[w]
                for t in range(NT):
                    o = pe.transpose(dst[:, t * P:(t + 1) * P], oT[:, t * P:(t + 1) * P], ident[:, :])
                o.then_inc(s_oTT, 1)

            def gather_turn(e):
                pe.wait_ge(s_g, 16 * (e + 1))
                for k in range(KC):
                    o = pe.transpose(psX[:, k // 4, (k % 4) * P:(k % 4 + 1) * P], xg[:, k * P:(k + 1) * P],
                                     ident[:, :])
                o.then_inc(s_gT, 1)

            def hidden_mm(e):
                pe.wait_ge(s_glo, e + 1)
                for c in range(4):
                    pe.wait_ge(s_ewlo, PIECES * e + c + 1)
                    for kk in range(PK):
                        k = PK * c + kk
                        for w in range(2):
                            cols = slice((2 * kk + w) * FF, (2 * kk + w + 1) * FF)
                            o = three(psH[:, w, 0:FF], gT_hi[:, k, :], gT_lo[:, k, :], ew_hi[:, c % 3, cols],
                                      ew_lo[:, c % 3, cols], k == 0, k == KC - 1)
                    o.then_inc(s_ewu, 1)

            def hidden_turn(e):
                pe.wait_ge(s_hh, e + 1)
                for f in range(FC):
                    o = pe.transpose(psX[:, 0, f * P:(f + 1) * P], hh[:, f * P:(f + 1) * P], ident[:, :])
                o.then_inc(s_hT, 1)

            def output_mm(e):
                pe.wait_ge(s_hlo, e + 1)
                for h in range(2):
                    c = 4 + h
                    pe.wait_ge(s_ewlo, PIECES * e + c + 1)
                    for f in range(FC):
                        cols = slice(f * TB, (f + 1) * TB)
                        o = three(psY[:, h, :], hT_hi[:, f, :], hT_lo[:, f, :], ew_hi[:, c % 3, cols],
                                  ew_lo[:, c % 3, cols], f == 0, f == FC - 1)
                    o.then_inc(s_ewu, 1)

            def token_sums(j):
                pe.wait_ge(s_sum, KC * (j + 1) + 1)
                pe.wait_ge(s_vq, 16 * j + 16 + 1)
                pe.wait_ge(s_go, 16 * j + 8 + 2)
                for i, t in enumerate((y_sum, q_sum)):
                    for s in range(NT):
                        o = pe.matmul(psA[:, 0, i * NT + s:i * NT + s + 1], t[:, s * P:(s + 1) * P],
                                      ones[:, 0:1], start=True, stop=True)
                o.then_inc(s_smm, 1)

            def token_spread(j):
                pe.wait_ge(s_dg, j + 1)
                pe.matmul(psA[:, 0, :], ones[:, :], dg_mu[:, :, :].rearrange("p t c -> p (t c)"),
                          start=True, stop=True)
                pe.matmul(psA[:, 1, :], ones[:, :], dg_rs[:, :, :].rearrange("p t c -> p (t c)"),
                          start=True, stop=True).then_inc(s_bc, 1)

            def run(j, e0, last):
                with_e = e0 is not None
                if with_e:
                    wait_alone(pe, s_xlo, 4 * j)

                def qvg(mm):
                    if with_e:
                        e = e0 + mm
                        hidden_mm(e)
                    qvg_proj(j, mm, 0)
                    qvg_proj(j, mm, 1)
                    if with_e:
                        hidden_turn(e)
                    qvg_proj(j, mm, 2)
                    if with_e:
                        output_mm(e)
                        gather_turn(e + 1)
                    qvg_proj(j, mm, 3)
                    qvg_proj(j, mm, 4)
                    qvg_proj(j, mm, 5)

                each_qvg(pe, qvg)
                if with_e:
                    hidden_mm(e0 + 4)
                token_sums(j)
                token_spread(j)
                if with_e:
                    hidden_turn(e0 + 4)
                    output_mm(e0 + 4)
                    gather_turn(e0 + 5)

                def outp(mm, loads, splits):
                    if with_e:
                        e = e0 + 5 + mm
                        hidden_mm(e)
                    out_proj(j, mm, 0)
                    if with_e:
                        hidden_turn(e)
                    out_turn(j, mm, 0)
                    if not last:
                        pe.wait_ge(s_xnl, 16 * (4 * j + mm + 1))
                        for k in range(KC):
                            o = pe.transpose(psH[:, k // 4, (k % 4) * P:(k % 4 + 1) * P],
                                             xn[:, k * P:(k + 1) * P], ident[:, :])
                        o.then_inc(s_xT, 1)
                    if with_e:
                        output_mm(e)
                        pe.wait_ge(s_ot, KC * j + 2 * mm + 1)
                        gather_turn(e + 1)
                    out_proj(j, mm, 1)
                    if with_e:
                        pe.wait_ge(s_ys, e + 1)
                    out_turn(j, mm, 1)

                each_out(pe, last, outp)
                if not with_e:
                    pe.wait_ge(s_lf, 1 + SLOTS // 8)
                    pe.wait_ge(s_ot, KC)
                    pe.transpose(psX[:, 0, 0:SEL], lf[:, :], ident[0:SEL, 0:SEL]).then_inc(s_lfT, 1)
                    pe.wait_ge(s_ix, 5)
                    gather_turn(0)

            phases(pe, run)
            hidden_mm(experts - 1)
            hidden_turn(experts - 1)
            output_mm(experts - 1)


def kernel(L0_attn_x, L0_attn_Wq, L0_attn_Wv, L0_attn_Wg, L0_attn_Wo, L0_attn_beta, L0_attn_ln_g,
           L0_attn_ln_b, L0_ffn_router_w, L0_ffn_w1, L0_ffn_v1, L0_ffn_w2):
    import concourse.bacc as bacc
    from concourse.bass_utils import run_bass_kernel_spmd

    B, S, D = L0_attn_x.shape
    E, F, _ = L0_ffn_w1.shape
    K, H = D // P, L0_attn_beta.shape[0]
    NB = B * S // TB

    cut = lambda w: np.asarray(w).reshape(K, P, K, P).transpose(2, 1, 0, 3)
    vqg = np.stack([cut(L0_attn_Wv), cut(L0_attn_Wq), cut(L0_attn_Wg)], axis=1).reshape(3 * K, P, K * P)
    steps = np.concatenate([vqg, cut(L0_attn_Wo).reshape(K, P, K * P)])
    steps = np.ascontiguousarray(np.concatenate([steps, steps[:4]]))
    up = np.stack([np.asarray(L0_ffn_w1), np.asarray(L0_ffn_v1)], axis=1)
    up = up.reshape(E, 2, F, 4, K // 4, P).transpose(0, 3, 5, 4, 1, 2).reshape(E, 4, P, -1)
    down = np.asarray(L0_ffn_w2).reshape(E, F // P, P, 2, D // 2).transpose(0, 3, 2, 1, 4).reshape(E, 2, P, -1)
    ew = np.concatenate([up, down], axis=1)
    router = np.zeros((P, K, SEL), np.float32)
    router[:, :, :E] = np.asarray(L0_ffn_router_w).reshape(E, K, P).transpose(2, 1, 0)
    per_part = lambda v: np.ascontiguousarray(np.asarray(v).reshape(K, P).T)
    beta = np.ascontiguousarray(np.repeat(np.asarray(L0_attn_beta), D // H).reshape(K, P).T)
    arrays = {
        "x": np.ascontiguousarray(np.asarray(L0_attn_x).reshape(B * S, D)), "proj_w": steps, "ew": ew,
        "router": router, "beta": beta, "ln_g": per_part(L0_attn_ln_g), "ln_b": per_part(L0_attn_ln_b),
    }
    nc = bacc.Bacc("TRN2", target_bir_lowering=False, num_devices=1)
    aps = {n: nc.dram_tensor(n + "_dram", a.shape, F32, kind="ExternalInput").ap() for n, a in arrays.items()}
    out = nc.dram_tensor("out_dram", (B * S, D), F32, kind="ExternalOutput").ap()
    build(nc, aps["x"], aps["proj_w"], aps["ew"], aps["router"], aps["beta"], aps["ln_g"], aps["ln_b"], out,
          B, S, E)
    r = run_bass_kernel_spmd(nc, [{n + "_dram": a for n, a in arrays.items()}], core_ids=[0])
    return r.results[0]["out_dram"].reshape(B, S, D)
```

```python
from contextlib import ExitStack

import numpy as np
import concourse.bass as bass
from concourse import mybir

F32 = mybir.dt.float32
F32R = mybir.dt.float32r
I32 = mybir.dt.int32
ALU = mybir.AluOpType
ACT = mybir.ActivationFunctionType
AX_X = mybir.AxisListType.X

P = 128
TB = 512
NT = TB // P
SLOTS = 128
TOPK = 8
SEL = 64
EPB = 9
PIECES = 6
NEG = -3.0e38
EPS = 1e-5


def build(nc, x, proj_w, ew, router, lam_in, g_in, b_in, out, batches, seq, experts):
    D = x.shape[1]
    KC = D // P
    FF = ew.shape[3] * 4 // (KC * 2)
    FC = FF // P
    NTOK = batches * seq
    NB = NTOK // TB
    assert seq == 2 * TB and KC == 8 and experts == (NB - 1) * EPB + 1 and experts <= SEL
    PW = ew.shape[3]
    PK = KC // 4
    assert PW == PK * 2 * FF == FC * (D // 2)
    XW = D + SEL
    HT = 2 * TB * batches
    NPJ = 4 * KC
    RN = 1.0 / D

    ctx = ExitStack()
    with ctx:
        sem_of = {}

        def sem(name):
            sem_of[name] = ctx.enter_context(nc.semaphore(name))
            return sem_of[name]

        top = [0]
        slab_bytes = 203 * 1024
        slab = ctx.enter_context(nc.sbuf_tensor("slab", [P, slab_bytes // 4], F32))
        slab_at = nc.sbuf_base - slab_bytes

        def place(name, shape, dt, at=None):
            size = int(np.prod(shape[1:])) * 4
            if at is None:
                at = top[0]
                top[0] += size
            assert at + size <= slab_bytes, (name, at, size)
            t = nc.alloc_sbuf_tensor_at(name, shape, dt, offset=slab_at + at, align_bytes=4)
            return t

        ident = place("ident", [P, P], F32)
        ones = place("ones", [P, P], F32)
        lam = place("lam", [P, KC], F32)
        ln_g = place("ln_g", [P, KC], F32)
        ln_b = place("ln_b", [P, KC], F32)
        keep = place("keep", [P, NB], F32)
        carry = place("carry", [P, KC], F32)
        start = place("start", [P, KC], F32)
        idx = place("idx", [P, SEL], I32)
        g_idx = place("g_idx", [P, 1], I32)
        s_idx = place("s_idx", [P, 1], I32)
        w_tab = place("w_tab", [P, SEL], F32)
        col = place("col", [P, 6, NT], F32)
        col_hi = place("col_hi", [P, 2, NT], F32R)
        half = place("half", [P, 4], F32)
        xT_hi = place("xT_hi", [P, KC, TB], F32R)
        xT_lo = place("xT_lo", [P, KC, TB], F32R)
        at_y = top[0]
        yb = place("yb", [P, KC, TB], F32)
        z_lo = place("z_lo", [P, KC, TB], F32R, at_y)
        at_g = top[0]
        gb = place("gb", [P, KC, TB], F32)
        z_hi = place("z_hi", [P, KC, TB], F32R, at_g)
        pw_raw = place("pw_raw", [P, 2, KC, P], F32)
        pw_hi = place("pw_hi", [P, 2, KC, P], F32R)
        pw_lo = place("pw_lo", [P, 2, KC, P], F32R)
        st = place("st", [P, TB], F32)
        sq = place("sq", [P, TB], F32)
        y_sum = place("y_sum", [P, TB], F32)
        q_sum = place("q_sum", [P, TB], F32)
        tok6 = place("tok6", [P, NT, P], F32)
        tok6T = place("tok6T", [P, TB], F32R)
        ln6T = place("ln6T", [P, KC, P], F32R)
        xn = place("xn", [P, D], F32)
        ot = place("ot", [P, NT, 2 * P], F32)
        at_e = top[0]
        ew_raw = place("ew_raw", [P, 3, PW], F32)
        ew_hi = place("ew_hi", [P, 3, PW], F32R)
        ew_lo = place("ew_lo", [P, 3, PW], F32R)
        xg = place("xg", [P, XW], F32)
        gT_hi = place("gT_hi", [P, KC, P], F32R)
        gT_lo = place("gT_lo", [P, KC, P], F32R)
        sh = place("sh", [P, FF], F32)
        hh = place("hh", [P, FF], F32)
        hT_hi = place("hT_hi", [P, FC, P], F32R)
        hT_lo = place("hT_lo", [P, FC, P], F32R)
        ys = place("ys", [P, D], F32)
        end_e = top[0]
        top[0] = at_e
        xt = place("xt", [P, 8, D], F32)
        keys = place("keys", [P, HT // 2], F32)
        key_base = place("key_base", [P, HT // 2], F32)
        key_iota = place("key_iota", [P, HT // 2], I32, top[0] - HT * 4)
        r_raw = place("r_raw", [P, KC, SEL], F32)
        r_hi = place("r_hi", [P, KC, P], F32R)
        r_lo = place("r_lo", [P, KC, P], F32R)
        lgT = place("lgT", [SEL, TB], F32)
        lg = place("lg", [P, NT, SEL], F32)
        shf = place("shf", [P, NT, SEL], F32)
        ex = place("ex", [P, NT, SEL], F32)
        rep = place("rep", [P, NT, SEL], F32)
        mk = place("mk", [P, NT, 2 * SEL], F32)
        wt = place("wt", [P, 2, NT, SEL], F32)
        m8 = place("m8", [P, NT, 8], F32)
        bn = place("bn", [P, 2, NT, 2, 6], F32)
        mv = place("mv", [P, 2, NT, 2], F32)
        ve = place("ve", [P, NT], F32)
        rs = place("rs", [P, NT], F32)
        sm = place("sm", [P, 2, NT], F32)
        nmr = place("nmr", [P, NT], F32)
        top8 = place("top8", [P, 8], F32)
        ln2 = place("ln2", [P, 2, KC], F32)
        ln2_hi = place("ln2_hi", [P, 2, KC], F32R)
        ln6 = place("ln6", [P, KC, P], F32)
        l1 = place("l1", [P, SLOTS], F32)
        l2 = place("l2", [SEL, 2 * SLOTS], F32)
        lf = place("lf", [SEL, SLOTS], F32)
        ka = place("ka", [P, SEL], I32)
        kb = place("kb", [P, SEL], I32)
        kc = place("kc", [P, SEL], I32)
        assert top[0] <= end_e, (top[0], end_e)

        psX = ctx.enter_context(nc.psum_tensor("psX", [P, 2, TB], F32))
        psH = ctx.enter_context(nc.psum_tensor("psH", [P, 2, TB], F32))
        psY = ctx.enter_context(nc.psum_tensor("psY", [P, 2, TB], F32))
        psA = ctx.enter_context(nc.psum_tensor("psA", [P, 2, TB], F32))
        chunks = lambda ps: ps[:, :, :].rearrange("p a (b c) -> p (a b) c", c=P)

        scratch = nc.dram_tensor("xn_scratch", (NTOK + P, XW), F32).ap()

        s_par = sem("s_par")
        s_const = sem("s_const")
        s_vconst = sem("s_vconst")
        s_lam = sem("s_lam")
        s_rhi, s_rlo = sem("s_rhi"), sem("s_rlo")
        s_xld = [sem(f"s_xld{u}") for u in range(8)]
        s_xst = [sem(f"s_xst{u}") for u in range(8)]
        s_wst = sem("s_wst")
        s_wtf = sem("s_wtf")
        s_spare = sem("s_spare")
        s_x0 = sem("s_x0")
        s_bn = sem("s_bn")
        s_nm = sem("s_nm")
        s_rs = sem("s_rs")
        s_xn = sem("s_xn")
        s_pT = sem("s_pT")
        s_phi, s_plo = sem("s_phi"), sem("s_plo")
        s_rt = sem("s_rt")
        s_lgT = sem("s_lgT")
        s_lt = sem("s_lt")
        s_shf = sem("s_shf")
        s_ex = sem("s_ex")
        s_tk = sem("s_tk")
        s_mk = sem("s_mk")
        s_wm = sem("s_wm")
        s_mT = sem("s_mT")
        s_key = sem("s_key")
        s_ext = sem("s_ext")
        s_l1 = sem("s_l1")
        s_l2 = sem("s_l2")
        s_mrg = sem("s_mrg")
        s_lf = sem("s_lf")
        s_lfT = sem("s_lfT")
        s_ix = sem("s_ix")
        s_pw = [sem(f"s_pw{u}") for u in range(2)]
        s_pwhi, s_pwlo = sem("s_pwhi"), sem("s_pwlo")
        s_pj = sem("s_pj")
        s_vq = sem("s_vq")
        s_go = sem("s_go")
        s_car = sem("s_car")
        s_st0 = sem("s_st0")
        s_sq = sem("s_sq")
        s_sum0 = sem("s_sum0")
        s_sum = sem("s_sum")
        s_smm = sem("s_smm")
        s_col = sem("s_col")
        s_rsy = sem("s_rsy")
        s_tT = sem("s_tT")
        s_t6 = sem("s_t6")
        s_ln = sem("s_ln")
        s_lnT = sem("s_lnT")
        s_l6 = sem("s_l6")
        s_sh = sem("s_sh")
        s_z = sem("s_z")
        s_zhi, s_zlo = sem("s_zhi"), sem("s_zlo")
        s_zlo7 = sem("s_zlo7")
        s_acc = sem("s_acc")
        s_otf = sem("s_otf")
        s_xnl = sem("s_xnl")
        s_xT = sem("s_xT")
        s_xhi, s_xlo = sem("s_xhi"), sem("s_xlo")
        s_ew = [sem(f"s_ew{u}") for u in range(3)]
        s_ewhi, s_ewlo = sem("s_ewhi"), sem("s_ewlo")
        s_ewu = sem("s_ewu")
        s_gi = sem("s_gi")
        s_g = sem("s_g")
        s_w = sem("s_w")
        s_gT = sem("s_gT")
        s_ghi, s_glo = sem("s_ghi"), sem("s_glo")
        s_si = sem("s_si")
        s_hh = sem("s_hh")
        s_hT = sem("s_hT")
        s_hhi, s_hlo = sem("s_hhi"), sem("s_hlo")
        s_ys = sem("s_ys")
        s_sci = sem("s_sci")
        s_sc = sem("s_sc")
        s_ysf = sem("s_ysf")

        s_passed = sem("s_passed")

        N_PAR = 4
        TKS = 7
        CS = 7

        def n1(j, mm, a):
            return NPJ * j + 6 * mm + a

        def half1(j, mm, a):
            return (NPJ // 2) * j + 3 * mm + a // 2

        def n2(j, mm, w):
            return NPJ * j + 3 * KC + 2 * mm + w

        def half2(j, mm):
            return (NPJ // 2) * j + 3 * KC // 2 + mm

        def phases(eng, block):
            block(0, None, False)
            with eng.Fori(1, NB - 1) as j:
                block(j, EPB * (j - 1), False)
            block(NB - 1, EPB * (NB - 2), True)

        def each_qvg(eng, body):
            with eng.Fori(0, KC // 2) as mm:
                body(mm)

        def each_out(eng, last, body):
            if last:
                with eng.Fori(0, KC // 2 - 2) as mm:
                    body(mm, True, True)
                body(KC // 2 - 2, False, True)
                body(KC // 2 - 1, False, False)
            else:
                with eng.Fori(0, KC // 2) as mm:
                    body(mm, True, True)

        def row_of(pp, h, s):
            return (NB - 1 - h) * TB + s * P - pp * (2 * TB)

        def wait_alone(eng, semaphore, value):
            eng.wait_ge(semaphore, value)
            eng.sem_inc(s_passed, 1)

        block = ctx.enter_context(nc.Block())

        @block.sync
        def _(sp):
            sp.sem_inc(s_wtf, 2)
            sp.dma_start(lam[:, :], lam_in).then_inc(s_par, 16)
            sp.dma_start(ln_g[:, :], g_in).then_inc(s_par, 16)
            sp.dma_start(ln_b[:, :], b_in).then_inc(s_par, 16)
            sp.dma_start(r_raw[:, :, :], router).then_inc(s_par, 16)

            def load_x(row, u):
                sp.dma_start(xt[:, u, :], x[bass.ds(row, P), :]).then_inc(s_xld[u], 16)

            for u in range(8):
                load_x(row_of(0, u // NT, u % NT), u)

            def copy_x(b):
                sp.dma_start(out[bass.ds(b * TB, TB), :], x[bass.ds(b * TB, TB), :]).then_inc(s_x0, 16)

            def router_pair(pp, more):
                def store(h):
                    for s in range(NT):
                        u = NT * h + s
                        wait_alone(sp, s_xn, 8 * pp + u + 1)
                        sp.dma_start(scratch[bass.ds(row_of(pp, h, s), P), 0:D],
                                     xt[:, u, :]).then_inc(s_xst[u], 16)

                def reload(h):
                    for s in range(NT):
                        u = NT * h + s
                        sp.wait_ge(s_xst[u], 16 * (pp + 1))
                        wait_alone(sp, s_pT, 8 * pp + u + 1)
                        load_x(row_of(pp + 1, h, s), u)

                def store_w(h):
                    wait_alone(sp, s_wm, 2 * pp + h + 1)
                    for s in range(NT):
                        sp.dma_start(scratch[bass.ds(row_of(pp, h, s), P), D:XW],
                                     wt[:, h, s, :]).then_inc(s_wst, 16)
                    sp.wait_ge(s_wst, 16 * NT * (2 * pp + h + 1))
                    sp.sem_inc(s_wtf, 1)

                store(0)
                store(1)
                if more:
                    reload(0)
                copy_x(2 * pp)
                store_w(0)
                if more:
                    reload(1)
                copy_x(2 * pp + 1)
                store_w(1)

            def load_proj(slot, row, n_prev=None):
                if n_prev is not None:
                    sp.wait_ge(s_pwlo, n_prev)
                sp.dma_start(pw_raw[:, slot, :, :].rearrange("p k c -> p (k c)"),
                             proj_w[row, :, :]).then_inc(s_pw[slot], 16)

            def load_piece(e, c, n_prev=None):
                if n_prev is not None:
                    sp.wait_ge(s_ewlo, n_prev)
                sp.dma_start(ew_raw[:, c % 3, :], ew[e, c, :, :]).then_inc(s_ew[c % 3], 16)

            def load_xn(row):
                sp.dma_start(xn[:, :], scratch[bass.ds(row, P), 0:D]).then_inc(s_xnl, 16)

            def load_rest(e):
                for c in range(3):
                    load_piece(e, 3 + c, PIECES * e + 1 + c)

            def load_first(e):
                for c in range(3):
                    load_piece(e, c, PIECES * e - 2 + c)

            load_proj(0, 0)
            load_proj(1, 1)
            with sp.Fori(0, NB // 2 - 1) as pp:
                router_pair(pp, True)
            router_pair(NB // 2 - 1, False)
            sp.dma_start(scratch[NTOK:NTOK + P, 0:D], xt[:, 0, :]).then_inc(s_spare, 16)
            sp.dma_start(scratch[NTOK:NTOK + P, D:XW], wt[:, 0, 0, :]).then_inc(s_spare, 16)
            load_proj(0, 2, 1)
            load_proj(1, 3, 2)

            def run(j, e0, last):
                with_e = e0 is not None

                def qvg(mm):
                    for a in range(2, 6):
                        load_proj(a % 2, 6 * mm + a + 2, n1(j, mm, a) + 1)
                    if with_e:
                        load_rest(e0 + mm + 1)
                    for a in range(6, 8):
                        load_proj(a % 2, 6 * mm + a + 2, n1(j, mm, a) + 1)
                    if with_e:
                        load_first(e0 + mm + 2)

                each_qvg(sp, qvg)
                if with_e:
                    load_rest(e0 + 5)
                    load_first(e0 + 6)
                else:
                    sp.wait_ge(s_l1, SLOTS // 8)
                    sp.dma_start(l2[:, SLOTS:2 * SLOTS], l1[SEL:2 * SEL, :]).then_inc(s_l2, 16)
                    for u in range(8):
                        sp.wait_ge(s_xst[u], 16 * (NB // 2))
                    sp.wait_ge(s_spare, 32)
                    load_xn(TB)

                def outp(mm, loads, splits):
                    if not last:
                        sp.wait_ge(s_xT, 4 * j + mm + 1)
                        load_xn((j + 1) * TB + (mm + 1) * P)
                    if with_e:
                        load_rest(e0 + 6 + mm)
                    for w in range(2, 4):
                        if loads:
                            load_proj(w % 2, 3 * KC + 2 * mm + w + 2, n2(j, mm, w) + 1)
                    if with_e and splits:
                        load_first(e0 + 7 + mm)

                each_out(sp, last, outp)
                if not with_e:
                    sp.wait_ge(s_ix, 5)
                    for u in range(8):
                        sp.wait_ge(s_xst[u], 16 * (NB // 2))
                    for c in range(3):
                        load_piece(0, c)
                    load_rest(0)
                    load_first(1)

            phases(sp, run)

        @block.gpsimd
        def _(pool):
            pool.sem_inc(s_sum, 1)
            pool.sem_inc(s_otf, 1)
            pool.sem_inc(s_ysf, 1)
            pool.memset(ident[:, :], 0.0).then_inc(s_const, 1)
            for h in range(2):
                pool.wait_ge(s_const, h + 1)
                pool.iota(key_iota[h * SEL:(h + 1) * SEL, :], pattern=[[-1, HT // 2]],
                          base=HT - h * (HT // 2), channel_multiplier=0).then_inc(s_const, 1)
            pool.wait_ge(s_const, 3)
            pool.affine_select(out=ident[:, :], in_=ident[:, :], compare_op=ALU.not_equal, fill=1.0, base=0,
                               pattern=[[-1, P]], channel_multiplier=1).then_inc(s_const, 1)
            pool.wait_ge(s_const, 4)
            pool.tensor_copy(key_base[:, :], key_iota[:, :]).then_inc(s_const, 1)

            pool.wait_ge(s_vconst, 1)
            with pool.Fori(0, NB) as qq:
                pool.wait_ge(s_bn, 3 * qq + 3)
                pool.tensor_tensor(rs[:, :], ve[:, :], half[:, 0:NT], ALU.pow).then_inc(s_rs, 1)

            def gather(e):
                pool.tensor_copy(g_idx[:, :], idx[:, bass.ds(e, 1)]).then_inc(s_gi, 1)
                wait_alone(pool, s_gi, e + 1)
                pool.indirect_dma_start(xg[:, :], None, scratch,
                                        bass.IndirectOffsetOnAxis(ap=g_idx[:, 0:1], axis=0)
                                        ).then_inc(s_g, 16)

            def gather_next(e):
                pool.wait_ge(s_gT, e + 1)
                pool.wait_ge(s_w, e + 1)
                gather(e + 1)

            def scatter(e):
                pool.tensor_copy(s_idx[:, :], idx[:, bass.ds(e, 1)]).then_inc(s_sci, 1)
                pool.wait_ge(s_sci, e + 1)
                wait_alone(pool, s_ys, e + 1)
                pool.indirect_dma_start(out, bass.IndirectOffsetOnAxis(ap=s_idx[:, 0:1], axis=0),
                                        ys[:, :], None, compute_op=ALU.add).then_inc(s_sc, 16)
                pool.wait_ge(s_sc, 16 * (e + 1))
                pool.sem_inc(s_ysf, 1)

            def add_sums(j, mm, h):
                i = KC * j + 2 * mm + h
                pool.wait_ge(s_sq, i + 1)
                pool.wait_ge(s_sum, i + 1)
                pool.tensor_tensor(y_sum[:, :], y_sum[:, :], yb[:, 2 * mm + h, :], ALU.add)
                pool.tensor_tensor(q_sum[:, :], q_sum[:, :], sq[:, :], ALU.add).then_inc(s_sum, 1)

            def run(j, e0, last):
                with_e = e0 is not None
                if with_e:
                    wait_alone(pool, s_smm, j)
                pool.memset(y_sum[:, :], 0.0)
                pool.memset(q_sum[:, :], 0.0).then_inc(s_sum0, 1)
                wait_alone(pool, s_sum0, j + 1)

                def qvg(mm):
                    if with_e:
                        gather_next(e0 + mm)
                    add_sums(j, mm, 0)
                    if with_e:
                        scatter(e0 + mm)
                    add_sums(j, mm, 1)

                each_qvg(pool, qvg)
                if with_e:
                    gather_next(e0 + 4)
                pool.wait_ge(s_col, CS * j + 4)
                pool.tensor_tensor(col[:, 4, :], col[:, 3, :], half[:, 0:NT], ALU.pow).then_inc(s_rsy, 1)
                if with_e:
                    e = e0 + 5
                    pool.wait_ge(s_ewhi, PIECES * e + 2)
                    pool.wait_ge(s_ewlo, PIECES * e + 1)
                    pool.tensor_tensor(ew_lo[:, 1, :], ew_raw[:, 1, :], ew_hi[:, 1, :].bitcast(F32),
                                       ALU.subtract).then_inc(s_ewlo, 1)
                for m in range(KC - 1):
                    pool.wait_ge(s_zhi, KC * j + m + 1)
                    pool.tensor_tensor(z_lo[:, m, :], yb[:, m, :], z_hi[:, m, :].bitcast(F32),
                                       ALU.subtract).then_inc(s_zlo, 1)
                if with_e:
                    scatter(e0 + 4)
                if not with_e:
                    pool.wait_ge(s_x0, 16 * NB)

                def outp(mm, loads, splits):
                    if with_e:
                        gather_next(e0 + 5 + mm)
                        scatter(e0 + 5 + mm)
                    pool.wait_ge(s_go, 16 * j + 8 + 2 * mm + 2 + 2)
                    pool.dma_start(out[bass.ds(j * TB, TB), bass.ds(mm * 2 * P, 2 * P)]
                                   .rearrange("(t p) c -> p t c", p=P), ot[:, :, :],
                                   accum_op=ALU.add).then_inc(s_acc, 16)
                    pool.wait_ge(s_acc, 16 * (4 * j + mm + 1))
                    pool.sem_inc(s_otf, 1)

                each_out(pool, last, outp)
                if not with_e:
                    pool.wait_ge(s_ix, 5)
                    pool.wait_ge(s_wst, 16 * NB * NT)
                    for u in range(8):
                        pool.wait_ge(s_xst[u], 16 * (NB // 2))
                    gather(0)

            phases(pool, run)
            scatter(experts - 1)

        @block.scalar
        def _(act):
            act.sem_inc(s_go, 2)
            act.wait_ge(s_par, 16 * N_PAR)
            act.activation(lam[:, :], lam[:, :], ACT.Sigmoid).then_inc(s_lam, 1)
            act.wait_ge(s_vconst, 1)
            act.activation(r_hi[:, :, 0:SEL], r_raw[:, :, :], ACT.Copy).then_inc(s_rhi, 1)

            act.wait_ge(s_lnT, 1)
            act.activation(ln6T[:, :, :], chunks(psX), ACT.Copy).then_inc(s_l6, 1)

            def normalize(pp, h):
                act.wait_ge(s_nm, 2 * pp + h + 1)
                for s in range(NT):
                    u = NT * h + s
                    act.activation(xt[:, u, :], xt[:, u, :], ACT.Identity, bias=nmr[:, s:s + 1],
                                   scale=rs[:, s:s + 1]).then_inc(s_xn, 1)

            def router_block(pp, h, more=True):
                q = 2 * pp + h
                dst = (z_hi, xT_hi)[h]
                for s in range(NT):
                    act.wait_ge(s_pT, NT * q + s + 1)
                    act.activation(dst[:, :, s * P:(s + 1) * P], chunks((psX, psH)[s % 2]),
                                   ACT.Copy).then_inc(s_phi, 1)
                if more:
                    normalize(pp + h, 1 - h)
                act.wait_ge(s_rt, q + 1)
                act.activation(lgT[:, :], psA[0:SEL, 0, :], ACT.Copy).then_inc(s_lgT, 1)
                act.wait_ge(s_shf, q + 1)
                act.activation(ex[:, :, :], shf[:, :, :], ACT.Exp).then_inc(s_ex, 1)

            normalize(0, 0)
            with act.Fori(0, NB // 2 - 1) as pp:
                router_block(pp, 0)
                router_block(pp, 1)
            router_block(NB // 2 - 1, 0)
            router_block(NB // 2 - 1, 1, more=False)

            def proj_hi(n, slot, hf, used):
                act.wait_ge(s_pw[slot], 16 * (hf + 1))
                if used is not None:
                    act.wait_ge(s_pj, used)
                act.activation(pw_hi[:, slot, :, :], pw_raw[:, slot, :, :], ACT.Copy).then_inc(s_pwhi, 1)

            def piece_hi(e, c, used=True):
                act.wait_ge(s_ew[c % 3], 16 * (2 * e + c // 3 + 1))
                if used:
                    act.wait_ge(s_ewu, PIECES * e + c - 2)
                act.activation(ew_hi[:, c % 3, :], ew_raw[:, c % 3, :], ACT.Copy).then_inc(s_ewhi, 1)

            def silu_h(e):
                act.wait_ge(s_ewu, PIECES * e + 4)
                act.activation(sh[:, :], psH[:, 0, 0:FF], ACT.Silu).then_inc(s_si, 1)

            def hT_hi_of(e):
                act.wait_ge(s_hT, e + 1)
                act.activation(hT_hi[:, :, :].rearrange("p f c -> p (f c)"), psX[:, 0, 0:FF],
                               ACT.Copy).then_inc(s_hhi, 1)

            def y_out(e, part=None):
                if part != 1:
                    act.wait_ge(s_w, e + 1)
                    act.wait_ge(s_ysf, e + 1)
                for h in range(2) if part is None else (part,):
                    wait_alone(act, s_ewu, PIECES * e + 5 + h)
                    o = act.activation(ys[:, h * TB:(h + 1) * TB], psY[:, h, :], ACT.Copy,
                                       scale=w_tab[:, bass.ds(e, 1)])
                if part != 0:
                    o.then_inc(s_ys, 1)

            def gT_hi_of(e):
                wait_alone(act, s_g, 16 * (e + 1))
                act.activation(w_tab[:, bass.ds(e, 1)], xg[:, bass.ds(e + D, 1)], ACT.Copy).then_inc(s_w, 1)
                act.wait_ge(s_gT, e + 1)
                act.activation(gT_hi[:, :, :], chunks(psX), ACT.Copy).then_inc(s_ghi, 1)

            def hidden_part(e, c0=3):
                for c in range(c0, PIECES):
                    piece_hi(e, c)
                silu_h(e)

            def square(j, mm, h):
                act.wait_ge(s_vq, 16 * j + 4 * mm + 2 * h + 3)
                act.wait_ge(s_sum, KC * j + 2 * mm + h + 1)
                act.activation(sq[:, :], yb[:, 2 * mm + h, :], ACT.Square).then_inc(s_sq, 1)

            def gate(j, mm, h):
                act.wait_ge(s_pj, n1(j, mm, 3 * h + 2) + 1)
                act.activation(gb[:, 2 * mm + h, :], psA[:, h, :], ACT.Silu).then_inc(s_go, 1)

            def rows6(j):
                act.wait_ge(s_tT, j + 1)
                act.activation(tok6T[:, :], psA[:, 1, :], ACT.Copy).then_inc(s_t6, 1)

            def z_his(j, i):
                for m in (2 * i, 2 * i + 1):
                    act.wait_ge(s_z, 2 * KC * j + 4 * i + 3 + m % 2)
                    act.activation(z_hi[:, m, :], yb[:, m, :], ACT.Copy).then_inc(s_zhi, 1)

            def out_copy(j, mm, w):
                act.wait_ge(s_pj, n2(j, mm, w) + 1)
                if w == 0:
                    act.wait_ge(s_otf, 4 * j + mm + 1)
                for t in (2 * w, 2 * w + 1):
                    o = act.activation(ot[:, t, :], psA[:, w, (t % 2) * 2 * P:(t % 2 + 1) * 2 * P], ACT.Copy,
                                       scale=col[:, 4, t:t + 1])
                o.then_inc(s_go, 1)

            for n in range(2):
                proj_hi(n, n, 0, None)

            def run(j, e0, last):
                with_e = e0 is not None

                def qvg(mm):
                    e = None if not with_e else e0 + mm
                    S = lambda a: proj_hi(None, a % 2, half1(j, mm, a), n1(j, mm, a) - 1)
                    S(2)
                    S(3)
                    if with_e:
                        hT_hi_of(e)
                        piece_hi(e + 1, 0)
                    square(j, mm, 0)
                    gate(j, mm, 0)
                    S(4)
                    if with_e:
                        y_out(e)
                        piece_hi(e + 1, 1)
                        piece_hi(e + 1, 2)
                        gT_hi_of(e + 1)
                    S(5)
                    S(6)
                    square(j, mm, 1)
                    gate(j, mm, 1)
                    S(7)
                    if with_e:
                        hidden_part(e + 1)

                each_qvg(act, qvg)
                if with_e:
                    e = e0 + 4
                    hT_hi_of(e)
                    piece_hi(e + 1, 0)
                rows6(j)
                if with_e:
                    y_out(e, 0)
                    piece_hi(e + 1, 1)
                    y_out(e, 1)
                    gT_hi_of(e + 1)
                z_his(j, 0)
                if with_e:
                    piece_hi(e + 1, 2)
                z_his(j, 1)
                if with_e:
                    piece_hi(e + 1, 3)
                z_his(j, 2)
                z_his(j, 3)
                if with_e:
                    hidden_part(e + 1, c0=4)

                def outp(mm, loads, splits):
                    e = None if not with_e else e0 + 5 + mm
                    if with_e:
                        hT_hi_of(e)
                    if not last:
                        act.wait_ge(s_xT, 4 * j + mm + 1)
                        act.activation(xT_hi[:, :, bass.ds(mm * P, P)], chunks(psH), ACT.Copy).then_inc(s_xhi, 1)
                    if with_e:
                        piece_hi(e + 1, 0)
                    out_copy(j, mm, 0)
                    if with_e:
                        y_out(e, 0)
                        piece_hi(e + 1, 1)
                        y_out(e, 1)
                        gT_hi_of(e + 1)
                        piece_hi(e + 1, 2)
                    if splits:
                        proj_hi(None, 0, half2(j, mm + 1), n2(j, mm, 1) + 1)
                        proj_hi(None, 1, half2(j, mm + 1), n2(j, mm, 1) + 1)
                    if with_e:
                        piece_hi(e + 1, 3)
                    out_copy(j, mm, 1)
                    if with_e:
                        hidden_part(e + 1, c0=4)

                each_out(act, last, outp)
                if not with_e:
                    for c in range(3):
                        piece_hi(0, c, used=False)
                    gT_hi_of(0)
                    hidden_part(0)

            phases(act, run)
            hT_hi_of(experts - 1)
            y_out(experts - 1)

        @block.vector
        def _(dve):
            dve.sem_inc(s_vq, 1)
            dve.memset(r_hi[:, :, :].bitcast(F32), 0.0)
            dve.memset(r_lo[:, :, :].bitcast(F32), 0.0)
            dve.memset(carry[:, :], 0.0).then_inc(s_car, 1)
            dve.memset(idx[:, :], 0)
            dve.memset(ones[:, :], 1.0)
            dve.memset(half[:, :], -0.5)
            dve.memset(wt[:, :, :, :], 0.0)
            for b in range(NB):
                dve.memset(keep[:, b:b + 1], float(b % 2))
            dve.memset(mk[:, :, :], 0.0)
            dve.memset(tok6[:, :, :], 0.0)
            dve.memset(ln6[:, :, :], 0.0).then_inc(s_vconst, 1)
            dve.wait_ge(s_vconst, 1)
            dve.wait_ge(s_par, 16 * N_PAR)
            dve.tensor_scalar(ln2[:, 0, :], ln_g[:, :], -1.0, None, ALU.mult)
            dve.tensor_copy(ln2[:, 1, :], ln_b[:, :]).then_inc(s_ln, 1)
            dve.wait_ge(s_ln, 1)
            dve.tensor_copy(ln2_hi[:, :, :], ln2[:, :, :]).then_inc(s_ln, 1)
            dve.wait_ge(s_ln, 2)
            six = ln6[:, :, 0:6].rearrange("p k (i r) -> p i k r", r=3)
            hi = ln2_hi[:, :, :].bitcast(F32)
            for r in (0, 2):
                dve.tensor_copy(six[:, :, :, r], hi)
            dve.tensor_tensor(six[:, :, :, 1], ln2[:, :, :], hi, ALU.subtract).then_inc(s_ln, 1)
            dve.wait_ge(s_rhi, 1)
            dve.tensor_tensor(r_lo[:, :, 0:SEL], r_raw[:, :, :], r_hi[:, :, 0:SEL].bitcast(F32),
                              ALU.subtract).then_inc(s_rlo, 1)

            def norm_block(pp, h):
                q = 2 * pp + h
                for s in range(NT):
                    dve.wait_ge(s_xld[NT * h + s], 16 * (pp + 1))
                    for i in range(2):
                        o = dve.bn_stats(bn[:, h, s, i, :], xt[:, NT * h + s, i * TB:(i + 1) * TB])
                o.then_inc(s_bn, 1)
                wait_alone(dve, s_bn, 3 * q + 1)
                for s in range(NT):
                    o = dve.bn_aggr(mv[:, h, s, :], bn[:, h, s, :, :].rearrange("p a b -> p (a b)"))
                o.then_inc(s_bn, 1)
                dve.wait_ge(s_bn, 3 * q + 2)
                dve.tensor_scalar(ve[:, :], mv[:, h, :, 1], EPS, None, ALU.add).then_inc(s_bn, 1)
                dve.wait_ge(s_rs, q + 1)
                dve.scalar_tensor_tensor(nmr[:, :], mv[:, h, :, 0], -1.0, rs[:, :], ALU.mult,
                                         ALU.mult).then_inc(s_nm, 1)

            def lows(pp, h):
                dst, hi = ((z_lo, z_hi), (xT_lo, xT_hi))[h]
                for s in range(NT):
                    dve.wait_ge(s_phi, NT * (2 * pp + h) + s + 1)
                    c = slice(s * P, (s + 1) * P)
                    dve.tensor_tensor(dst[:, :, c], chunks((psX, psH)[s % 2]), hi[:, :, c].bitcast(F32),
                                      ALU.subtract).then_inc(s_plo, 1)

            def top8_of(pp, h):
                q = 2 * pp + h
                E = experts
                own = lambda i: dve.wait_ge(s_tk, TKS * q + i)
                dve.wait_ge(s_lt, q + 1)
                dve.tensor_copy(lg[:, :, :], psA[:, 1, 0:NT * SEL].rearrange("p (s e) -> p s e", e=SEL)
                                ).then_inc(s_tk, 1)
                wait_alone(dve, s_tk, TKS * q + 1)
                for s in range(NT):
                    o = dve.max(m8[:, s, :], lg[:, s, 0:E])
                o.then_inc(s_tk, 1)
                own(2)
                dve.tensor_tensor(shf[:, :, :], lg[:, :, :], m8[:, :, 0:1].to_broadcast([P, NT, SEL]),
                                  ALU.subtract).then_inc(s_shf, 1)
                for s in range(NT):
                    o = dve.match_replace(rep[:, s, 0:E], m8[:, s, :], lg[:, s, 0:E], NEG)
                o.then_inc(s_tk, 1)
                own(3)
                m = mk[:, :, (1 - h) * SEL:(1 - h) * SEL + E]
                dve.tensor_scalar(m, rep[:, :, 0:E], NEG, None, ALU.is_equal).then_inc(s_tk, 1)
                own(4)
                dve.wait_ge(s_ex, q + 1)
                w = wt[:, h, :, 0:E]
                dve.wait_ge(s_wtf, q + 1)
                dve.tensor_tensor(w, ex[:, :, 0:E], m, ALU.mult).then_inc(s_tk, 1)
                own(5)
                dve.tensor_reduce(sm[:, 0, :], w, AX_X, ALU.add).then_inc(s_tk, 1)
                own(6)
                dve.reciprocal(sm[:, 1, :], sm[:, 0, :]).then_inc(s_tk, 1)
                own(7)
                dve.tensor_tensor(w, w, sm[:, 1, :].unsqueeze(2).to_broadcast([P, NT, E]),
                                  ALU.mult).then_inc(s_wm, 1)

            def keys_of(pp):
                wait_alone(dve, s_mT, pp + 1)
                b = batches - 1 - pp
                view = lambda t: t[:, :].rearrange("p (s b) -> p s b", b=batches)[:, :, bass.ds(b, 1)]
                dve.scalar_tensor_tensor(view(keys), psY[:, 0, :].unsqueeze(2), float(HT), view(key_base),
                                         ALU.mult, ALU.add).then_inc(s_key, 1)

            def pair(pp, more):
                lows(pp, 0)
                norm_block(pp, 1)
                top8_of(pp, 0)
                lows(pp, 1)
                if more:
                    norm_block(pp + 1, 0)
                top8_of(pp, 1)
                keys_of(pp)

            dve.wait_ge(s_const, 5)
            norm_block(0, 0)
            with dve.Fori(0, NB // 2 - 1) as pp:
                pair(pp, True)
            pair(NB // 2 - 1, False)

            def extract(src, into, n, steps, copied):
                dve.max(top8[0:src.shape[0], :], src).then_inc(steps, 1)
                dve.wait_ge(steps, 2 * n + 1)
                dve.tensor_copy(into[:, bass.ds(n * 8, 8)], top8[0:src.shape[0], :]).then_inc(copied, 1)
                dve.match_replace(src, top8[0:src.shape[0], :], src, -1.0).then_inc(steps, 1)
                wait_alone(dve, steps, 2 * n + 2)

            def proj_lo(n, slot):
                dve.wait_ge(s_pwhi, n + 1)
                dve.tensor_tensor(pw_lo[:, slot, :, :], pw_raw[:, slot, :, :], pw_hi[:, slot, :, :].bitcast(F32),
                                  ALU.subtract).then_inc(s_pwlo, 1)

            def piece_lo(e, c):
                dve.wait_ge(s_ewhi, PIECES * e + c + 1)
                dve.tensor_tensor(ew_lo[:, c % 3, :], ew_raw[:, c % 3, :], ew_hi[:, c % 3, :].bitcast(F32),
                                  ALU.subtract).then_inc(s_ewlo, 1)

            def hidden(e):
                dve.wait_ge(s_si, e + 1)
                dve.tensor_tensor(hh[:, :], psH[:, 1, 0:FF], sh[:, :], ALU.mult).then_inc(s_hh, 1)

            def hidden_part(e, c0=3):
                for c in range(c0, PIECES):
                    piece_lo(e, c)
                hidden(e)

            def hT_lo_of(e):
                dve.wait_ge(s_hhi, e + 1)
                dve.tensor_tensor(hT_lo[:, :, :].rearrange("p f c -> p (f c)"), psX[:, 0, 0:FF],
                                  hT_hi[:, :, :].rearrange("p f c -> p (f c)").bitcast(F32),
                                  ALU.subtract).then_inc(s_hlo, 1)

            def gT_lo_of(e):
                dve.wait_ge(s_ghi, e + 1)
                dve.tensor_tensor(gT_lo[:, :, :], chunks(psX), gT_hi[:, :, :].bitcast(F32),
                                  ALU.subtract).then_inc(s_glo, 1)

            def scan(j, mm, h):
                m = 2 * mm + h
                dve.wait_ge(s_pj, n1(j, mm, 3 * h) + 1)
                dve.tensor_tensor_scan(st[:, :], lam[:, bass.ds(m, 1)].to_broadcast([P, TB]), psA[:, h, :],
                                       start[:, bass.ds(m, 1)], ALU.mult, ALU.add).then_inc(s_vq, 1)

            def times_q(j, mm, h):
                m = 2 * mm + h
                dve.wait_ge(s_pj, n1(j, mm, 3 * h + 1) + 1)
                dve.wait_ge(s_vq, 16 * j + 4 * mm + 2 * h + 2)
                dve.tensor_tensor(yb[:, m, :], psA[:, 1 - h, :], st[:, :], ALU.mult).then_inc(s_vq, 1)
                dve.tensor_copy(carry[:, bass.ds(m, 1)], st[:, TB - 1:TB]).then_inc(s_car, 1)

            def z_of(j, i):
                pair = (2 * i, 2 * i + 1)
                for m in pair:
                    dve.wait_ge(s_sh, KC * j + m + 1)
                    dve.scalar_tensor_tensor(yb[:, m, :], yb[:, m, :], ln_g[:, m:m + 1], psA[:, m % 2, :],
                                             ALU.mult, ALU.add).then_inc(s_z, 1)
                for m in pair:
                    dve.wait_ge(s_z, 2 * KC * j + 4 * i + 1 + m % 2)
                    dve.tensor_tensor(yb[:, m, :], yb[:, m, :], gb[:, m, :], ALU.mult).then_inc(s_z, 1)

            def token_var(j):
                own = lambda i: dve.wait_ge(s_col, CS * j + i)
                dve.wait_ge(s_smm, j + 1)
                dve.tensor_scalar(col[:, 0:2, :], psA[:, 0, 0:2 * NT].rearrange("p (i t) -> p i t", t=NT),
                                  RN, None, ALU.mult).then_inc(s_col, 1)
                own(1)
                dve.tensor_tensor(col[:, 2, :], col[:, 0, :], col[:, 0, :], ALU.mult).then_inc(s_col, 1)
                own(2)
                dve.tensor_tensor(col[:, 2, :], col[:, 1, :], col[:, 2, :], ALU.subtract).then_inc(s_col, 1)
                own(3)
                dve.tensor_scalar(col[:, 3, :], col[:, 2, :], 0.0, EPS, ALU.max, ALU.add).then_inc(s_col, 1)

            def token_six(j):
                own = lambda i: dve.wait_ge(s_col, CS * j + i)
                dve.wait_ge(s_rsy, j + 1)
                dve.tensor_tensor(col[:, 1, :], col[:, 3, :], col[:, 4, :], ALU.mult).then_inc(s_col, 1)
                own(5)
                dve.tensor_copy(col_hi[:, :, :], col[:, 0:2, :]).then_inc(s_col, 1)
                own(6)
                six = tok6[:, :, 0:6].rearrange("p t (i r) -> p i t r", r=3)
                hi = col_hi[:, :, :].bitcast(F32)
                for r in range(2):
                    dve.tensor_copy(six[:, :, :, r], hi)
                dve.tensor_tensor(six[:, :, :, 2], col[:, 0:2, :], hi, ALU.subtract).then_inc(s_col, 1)

            for n in range(2):
                proj_lo(n, n)

            def run(j, e0, last):
                with_e = e0 is not None
                dve.wait_ge(s_car, KC * j + 1)
                dve.tensor_scalar(start[:, :], carry[:, :], keep[:, bass.ds(j, 1)], None,
                                  ALU.mult).then_inc(s_st0, 1)
                wait_alone(dve, s_st0, j + 1)
                if not with_e:
                    dve.wait_ge(s_key, NB // 2)
                    dve.wait_ge(s_lam, 1)

                def qvg(mm):
                    e = None if not with_e else e0 + mm
                    S = lambda a: proj_lo(n1(j, mm, a), a % 2)

                    def round_(r):
                        if not with_e:
                            extract(keys[:, :], l1, 4 * mm + r, s_ext, s_l1)

                    round_(0)
                    scan(j, mm, 0)
                    S(2)
                    round_(1)
                    times_q(j, mm, 0)
                    S(3)
                    if with_e:
                        hT_lo_of(e)
                        piece_lo(e + 1, 0)
                    round_(2)
                    S(4)
                    if with_e:
                        piece_lo(e + 1, 1)
                        piece_lo(e + 1, 2)
                        gT_lo_of(e + 1)
                    round_(3)
                    scan(j, mm, 1)
                    S(5)
                    times_q(j, mm, 1)
                    S(6)
                    S(7)
                    if with_e:
                        hidden_part(e + 1)

                each_qvg(dve, qvg)
                token_var(j)
                if with_e:
                    e = e0 + 4
                    hT_lo_of(e)
                else:
                    dve.wait_ge(s_l1, SLOTS // 8)
                    dve.tensor_copy(l2[:, 0:SLOTS], l1[0:SEL, :]).then_inc(s_lf, 1)
                token_six(j)
                if with_e:
                    piece_lo(e + 1, 0)
                z_of(j, 0)
                if with_e:
                    gT_lo_of(e + 1)
                z_of(j, 1)
                if with_e:
                    dve.wait_ge(s_ewlo, PIECES * (e + 1) + 2)
                    piece_lo(e + 1, 2)
                z_of(j, 2)
                if with_e:
                    piece_lo(e + 1, 3)
                z_of(j, 3)
                dve.wait_ge(s_zhi, KC * (j + 1))
                dve.tensor_tensor(z_lo[:, KC - 1, :], yb[:, KC - 1, :], z_hi[:, KC - 1, :].bitcast(F32),
                                  ALU.subtract).then_inc(s_zlo7, 1)
                if with_e:
                    hidden_part(e + 1, c0=4)
                if not with_e:
                    dve.wait_ge(s_l2, 16)
                    dve.wait_ge(s_lf, 1)

                def outp(mm, loads, splits):
                    if with_e:
                        e = e0 + 5 + mm
                        hT_lo_of(e)
                    else:
                        for r in range(4):
                            extract(l2[:, :], lf, 4 * mm + r, s_mrg, s_lf)
                    if not last:
                        dve.wait_ge(s_xhi, 4 * j + mm + 1)
                        c = bass.ds(mm * P, P)
                        dve.tensor_tensor(xT_lo[:, :, c], chunks(psH), xT_hi[:, :, c].bitcast(F32),
                                          ALU.subtract).then_inc(s_xlo, 1)
                    if with_e:
                        piece_lo(e + 1, 0)
                        gT_lo_of(e + 1)
                        piece_lo(e + 1, 1)
                        piece_lo(e + 1, 2)
                    if splits:
                        proj_lo(n2(j, mm, 2), 0)
                        proj_lo(n2(j, mm, 3), 1)
                    if with_e:
                        hidden_part(e + 1)

                each_out(dve, last, outp)
                if not with_e:
                    own = lambda i: dve.wait_ge(s_ix, i)
                    dve.wait_ge(s_lfT, 1)
                    dve.tensor_scalar(ka[:, :], psX[:, 0, 0:SEL], -1.0, float(2 * HT), ALU.mult,
                                      ALU.add).then_inc(s_ix, 1)
                    own(1)
                    dve.tensor_scalar(kb[:, :], ka[:, :], batches - 1, seq.bit_length() - 1, ALU.bitwise_and,
                                      ALU.logical_shift_left).then_inc(s_ix, 1)
                    own(2)
                    dve.tensor_scalar(kc[:, :], ka[:, :], HT - 1, batches.bit_length() - 1, ALU.bitwise_and,
                                      ALU.logical_shift_right).then_inc(s_ix, 1)
                    own(3)
                    dve.tensor_tensor(idx[:, 0:experts], kb[:, 0:experts], kc[:, 0:experts],
                                      ALU.add).then_inc(s_ix, 2)
                    for c in range(3):
                        piece_lo(0, c)
                    gT_lo_of(0)
                    hidden_part(0)

            phases(dve, run)
            hT_lo_of(experts - 1)

        @block.tensor
        def _(pe):
            def three(dst, l_hi, l_lo, r_hi_, r_lo_, first, last):
                pe.matmul(dst, l_hi, r_hi_, start=first, stop=False)
                pe.matmul(dst, l_hi, r_lo_, start=False, stop=False)
                return pe.matmul(dst, l_lo, r_hi_, start=False, stop=last)

            pe.wait_ge(s_const, 5)
            pe.wait_ge(s_vconst, 1)
            pe.wait_ge(s_rlo, 1)
            pe.wait_ge(s_ln, 3)
            for k in range(KC):
                o = pe.transpose(psX[:, k // 4, (k % 4) * P:(k % 4 + 1) * P], ln6[:, k, :], ident[:, :])
            o.then_inc(s_lnT, 1)
            pe.wait_ge(s_l6, 1)

            def router_block(pp, h):
                q = 2 * pp + h
                hi, lo = ((z_hi, z_lo), (xT_hi, xT_lo))[h]
                for s in range(NT):
                    pe.wait_ge(s_xn, NT * q + s + 1)
                    if s >= 2:
                        pe.wait_ge(s_plo, NT * q + s - 1)
                    bank = (psX, psH)[s % 2]
                    for k in range(KC):
                        o = pe.transpose(bank[:, k // 4, (k % 4) * P:(k % 4 + 1) * P],
                                         xt[:, NT * h + s, k * P:(k + 1) * P], ident[:, :])
                    o.then_inc(s_pT, 1)
                pe.wait_ge(s_plo, NT * q + NT)
                for k in range(KC):
                    three(psA[:, 0, :], r_hi[:, k, :], r_lo[:, k, :], hi[:, k, :], lo[:, k, :], k == 0, False)
                    o = pe.matmul(psA[:, 0, :], r_lo[:, k, :], lo[:, k, :], start=False, stop=k == KC - 1)
                o.then_inc(s_rt, 1)
                wait_alone(pe, s_lgT, q + 1)
                for s in range(NT):
                    o = pe.transpose(psA[:, 1, s * SEL:(s + 1) * SEL], lgT[:, s * P:(s + 1) * P],
                                     ident[0:SEL, 0:SEL])
                o.then_inc(s_lt, 1)

            with pe.Fori(0, NB // 2) as pp:
                router_block(pp, 0)
                router_block(pp, 1)
                pe.wait_ge(s_tk, TKS * (2 * pp + 1) + 4)
                for s in range(NT):
                    o = pe.transpose(psY[:, 0, s * P:(s + 1) * P], mk[:, s, :], ident[:, :])
                o.then_inc(s_mT, 1)

            def proj(n, bank, slot, hi, lo):
                pe.wait_ge(s_pwlo, n + 1)
                for k in range(KC):
                    o = three(psA[:, bank, :], pw_hi[:, slot, k, :], pw_lo[:, slot, k, :], hi[:, k, :],
                              lo[:, k, :], k == 0, k == KC - 1)
                o.then_inc(s_pj, 1)

            def qvg_proj(j, mm, a):
                vq = {0: 0, 2: 1, 3: 2, 5: 3}
                go = {0: -1, 1: 0, 4: 1}
                if a in vq:
                    pe.wait_ge(s_vq, 16 * j + 4 * mm + vq[a] + 1)
                if a in go:
                    pe.wait_ge(s_go, 16 * j + 2 * mm + go[a] + 2)
                proj(n1(j, mm, a), a % 2, a % 2, xT_hi, xT_lo)

            def out_proj(j, mm, w, tiles=(0, 1)):
                if 0 not in tiles:
                    pass
                elif w == 0:
                    pe.wait_ge(s_go, 16 * j + 7 + 2 * mm + 2)
                    pe.wait_ge(s_z, 2 * KC * j + 2 * KC - 3)
                    pe.wait_ge(s_zlo, (KC - 1) * j + KC - 2)
                    pe.wait_ge(s_pwlo, n2(j, mm, 1) + 1)
                else:
                    pe.wait_ge(s_go, 16 * j + 8 + 2 * mm + 2)
                for t in tiles:
                    c = slice((2 * w + t) * P, (2 * w + t + 1) * P)
                    for k in range(KC):
                        if w == 0 and t == 0 and k == KC - 2:
                            pe.wait_ge(s_zlo, (KC - 1) * (j + 1))
                        if w == 0 and t == 0 and k == KC - 1:
                            pe.wait_ge(s_zlo7, j + 1)
                        o = three(psA[:, w, t * 2 * P:(t + 1) * 2 * P], z_hi[:, k, c], z_lo[:, k, c],
                                  pw_hi[:, :, k, :], pw_lo[:, :, k, :], k == 0, k == KC - 1)
                if 1 in tiles:
                    o.then_inc(s_pj, 1)

            def gather_turn(e):
                pe.wait_ge(s_g, 16 * (e + 1))
                for k in range(KC):
                    o = pe.transpose(psX[:, k // 4, (k % 4) * P:(k % 4 + 1) * P], xg[:, k * P:(k + 1) * P],
                                     ident[:, :])
                o.then_inc(s_gT, 1)

            def hidden_mm(e, parts=range(4)):
                for c in parts:
                    if c == 0:
                        pe.wait_ge(s_glo, e + 1)
                    pe.wait_ge(s_ewlo, PIECES * e + c + 1)
                    for kk in range(PK):
                        k = PK * c + kk
                        for w in range(2):
                            cols = slice((2 * kk + w) * FF, (2 * kk + w + 1) * FF)
                            o = three(psH[:, w, 0:FF], gT_hi[:, k, :], gT_lo[:, k, :], ew_hi[:, c % 3, cols],
                                      ew_lo[:, c % 3, cols], k == 0, k == KC - 1)
                    o.then_inc(s_ewu, 1)

            def hidden_turn(e):
                pe.wait_ge(s_hh, e + 1)
                for f in range(FC):
                    o = pe.transpose(psX[:, 0, f * P:(f + 1) * P], hh[:, f * P:(f + 1) * P], ident[:, :])
                o.then_inc(s_hT, 1)

            def output_mm(e, halves=range(2)):
                for h in halves:
                    if h == 0:
                        pe.wait_ge(s_hlo, e + 1)
                    c = 4 + h
                    pe.wait_ge(s_ewlo, PIECES * e + c + 1)
                    for f in range(FC):
                        cols = slice(f * TB, (f + 1) * TB)
                        o = three(psY[:, h, :], hT_hi[:, f, :], hT_lo[:, f, :], ew_hi[:, c % 3, cols],
                                  ew_lo[:, c % 3, cols], f == 0, f == FC - 1)
                    o.then_inc(s_ewu, 1)

            def token_sums(j):
                pe.wait_ge(s_sum, KC * (j + 1) + 1)
                pe.wait_ge(s_vq, 16 * j + 16 + 1)
                pe.wait_ge(s_go, 16 * j + 8 + 2)
                for i, t in enumerate((y_sum, q_sum)):
                    for s in range(NT):
                        o = pe.matmul(psA[:, 0, i * NT + s:i * NT + s + 1], t[:, s * P:(s + 1) * P],
                                      ones[:, 0:1], start=True, stop=True)
                o.then_inc(s_smm, 1)

            def token_turn(j):
                pe.wait_ge(s_col, CS * j + 7)
                for t in range(NT):
                    o = pe.transpose(psA[:, 1, t * P:(t + 1) * P], tok6[:, t, :], ident[:, :])
                o.then_inc(s_tT, 1)

            def shifts(j, i):
                if i == 0:
                    pe.wait_ge(s_t6, j + 1)
                for m in (2 * i, 2 * i + 1):
                    if i > 0:
                        pe.wait_ge(s_z, 2 * KC * j + 4 * i - 3 + m % 2)
                    pe.matmul(psA[:, m % 2, :], ln6T[:, m, :], tok6T[:, :], start=True, stop=True
                              ).then_inc(s_sh, 1)

            def run(j, e0, last):
                with_e = e0 is not None
                if with_e:
                    wait_alone(pe, s_xlo, 4 * j)

                def qvg(mm):
                    e = None if not with_e else e0 + mm
                    qvg_proj(j, mm, 0)
                    qvg_proj(j, mm, 1)
                    if with_e:
                        hidden_turn(e)
                    qvg_proj(j, mm, 2)
                    if with_e:
                        output_mm(e)
                        gather_turn(e + 1)
                    qvg_proj(j, mm, 3)
                    qvg_proj(j, mm, 4)
                    qvg_proj(j, mm, 5)
                    if with_e:
                        hidden_mm(e + 1)

                each_qvg(pe, qvg)
                e = None if not with_e else e0 + 4
                token_sums(j)
                if with_e:
                    hidden_turn(e)
                    output_mm(e, (0,))
                token_turn(j)
                if with_e:
                    output_mm(e, (1,))
                shifts(j, 0)
                if with_e:
                    gather_turn(e + 1)
                for i in range(1, 4):
                    shifts(j, i)
                    if with_e:
                        hidden_mm(e + 1, (i - 1,))
                if with_e:
                    hidden_mm(e + 1, (3,))

                def outp(mm, loads, splits):
                    out_proj(j, mm, 0)
                    if with_e:
                        e = e0 + 5 + mm
                        hidden_turn(e)
                    if not last:
                        pe.wait_ge(s_xnl, 16 * (4 * j + mm + 1))
                        for k in range(KC):
                            o = pe.transpose(psH[:, k // 4, (k % 4) * P:(k % 4 + 1) * P],
                                             xn[:, k * P:(k + 1) * P], ident[:, :])
                        o.then_inc(s_xT, 1)
                    out_proj(j, mm, 1, (0,))
                    if with_e:
                        output_mm(e)
                        gather_turn(e + 1)
                    out_proj(j, mm, 1, (1,))
                    if with_e:
                        hidden_mm(e + 1)

                each_out(pe, last, outp)
                if not with_e:
                    pe.wait_ge(s_lf, 1 + SLOTS // 8)
                    pe.transpose(psX[:, 0, 0:SEL], lf[:, :], ident[0:SEL, 0:SEL]).then_inc(s_lfT, 1)
                    pe.wait_ge(s_ix, 5)
                    gather_turn(0)
                    hidden_mm(0)

            phases(pe, run)
            hidden_turn(experts - 1)
            output_mm(experts - 1)


def kernel(L0_attn_x, L0_attn_Wq, L0_attn_Wv, L0_attn_Wg, L0_attn_Wo, L0_attn_beta, L0_attn_ln_g,
           L0_attn_ln_b, L0_ffn_router_w, L0_ffn_w1, L0_ffn_v1, L0_ffn_w2):
    import concourse.bacc as bacc
    from concourse.bass_utils import run_bass_kernel_spmd

    B, S, D = L0_attn_x.shape
    E, F, _ = L0_ffn_w1.shape
    K, H = D // P, L0_attn_beta.shape[0]
    NB = B * S // TB

    cut = lambda w: np.asarray(w).reshape(K, P, K, P).transpose(2, 1, 0, 3)
    vqg = np.stack([cut(L0_attn_Wv), cut(L0_attn_Wq), cut(L0_attn_Wg)], axis=1).reshape(3 * K, P, K * P)
    steps = np.concatenate([vqg, cut(L0_attn_Wo).reshape(K, P, K * P)])
    steps = np.ascontiguousarray(np.concatenate([steps, steps[:4]]))
    up = np.stack([np.asarray(L0_ffn_w1), np.asarray(L0_ffn_v1)], axis=1)
    up = up.reshape(E, 2, F, 4, K // 4, P).transpose(0, 3, 5, 4, 1, 2).reshape(E, 4, P, -1)
    down = np.asarray(L0_ffn_w2).reshape(E, F // P, P, 2, D // 2).transpose(0, 3, 2, 1, 4).reshape(E, 2, P, -1)
    ew = np.concatenate([up, down], axis=1)
    router = np.zeros((P, K, SEL), np.float32)
    router[:, :, :E] = np.asarray(L0_ffn_router_w).reshape(E, K, P).transpose(2, 1, 0)
    per_part = lambda v: np.ascontiguousarray(np.asarray(v).reshape(K, P).T)
    beta = np.ascontiguousarray(np.repeat(np.asarray(L0_attn_beta), D // H).reshape(K, P).T)
    arrays = {
        "x": np.ascontiguousarray(np.asarray(L0_attn_x).reshape(B * S, D)), "proj_w": steps, "ew": ew,
        "router": router, "beta": beta, "ln_g": per_part(L0_attn_ln_g), "ln_b": per_part(L0_attn_ln_b),
    }
    nc = bacc.Bacc("TRN2", target_bir_lowering=False, num_devices=1)
    aps = {n: nc.dram_tensor(n + "_dram", a.shape, F32, kind="ExternalInput").ap() for n, a in arrays.items()}
    out = nc.dram_tensor("out_dram", (B * S, D), F32, kind="ExternalOutput").ap()
    build(nc, aps["x"], aps["proj_w"], aps["ew"], aps["router"], aps["beta"], aps["ln_g"], aps["ln_b"], out,
          B, S, E)
    r = run_bass_kernel_spmd(nc, [{n + "_dram": a for n, a in arrays.items()}], core_ids=[0])
    return r.results[0]["out_dram"].reshape(B, S, D)
```

```python
from contextlib import ExitStack

import numpy as np
import concourse.bass as bass
from concourse import mybir

F32 = mybir.dt.float32
F32R = mybir.dt.float32r
I32 = mybir.dt.int32
ALU = mybir.AluOpType
ACT = mybir.ActivationFunctionType
AX_X = mybir.AxisListType.X

P = 128
TB = 512
NT = TB // P
SLOTS = 128
TOPK = 8
SEL = 64
EPB = 9
PIECES = 6
NEG = -3.0e38
EPS = 1e-5


def build(nc, x, proj_w, ew, router, lam_in, g_in, b_in, out, batches, seq, experts):
    D = x.shape[1]
    KC = D // P
    FF = ew.shape[3] * 4 // (KC * 2)
    FC = FF // P
    NTOK = batches * seq
    NB = NTOK // TB
    assert seq == 2 * TB and KC == 8 and experts == (NB - 1) * EPB + 1 and experts <= SEL
    PW = ew.shape[3]
    PK = KC // 4
    assert PW == PK * 2 * FF == FC * (D // 2)
    XW = D + SEL
    HT = 2 * TB * batches
    NPJ = 4 * KC
    RN = 1.0 / D

    ctx = ExitStack()
    with ctx:
        sem_of = {}

        def sem(name):
            sem_of[name] = ctx.enter_context(nc.semaphore(name))
            return sem_of[name]

        top = [0]
        slab_bytes = 203 * 1024
        slab = ctx.enter_context(nc.sbuf_tensor("slab", [P, slab_bytes // 4], F32))
        slab_at = nc.sbuf_base - slab_bytes

        def place(name, shape, dt, at=None):
            size = int(np.prod(shape[1:])) * 4
            if at is None:
                at = top[0]
                top[0] += size
            assert at + size <= slab_bytes, (name, at, size)
            t = nc.alloc_sbuf_tensor_at(name, shape, dt, offset=slab_at + at, align_bytes=4)
            return t

        ident = place("ident", [P, P], F32)
        ones = place("ones", [P, P], F32)
        lam = place("lam", [P, KC], F32)
        ln_g = place("ln_g", [P, KC], F32)
        ln_b = place("ln_b", [P, KC], F32)
        keep = place("keep", [P, NB], F32)
        carry = place("carry", [P, KC], F32)
        start = place("start", [P, KC], F32)
        idx = place("idx", [P, SEL], I32)
        g_idx = place("g_idx", [P, 1], I32)
        s_idx = place("s_idx", [P, 1], I32)
        w_tab = place("w_tab", [P, SEL], F32)
        col = place("col", [P, 6, NT], F32)
        col_hi = place("col_hi", [P, 2, NT], F32R)
        half = place("half", [P, 4], F32)
        xT_hi = place("xT_hi", [P, KC, TB], F32R)
        xT_lo = place("xT_lo", [P, KC, TB], F32R)
        at_y = top[0]
        yb = place("yb", [P, KC, TB], F32)
        z_lo = place("z_lo", [P, KC, TB], F32R, at_y)
        at_g = top[0]
        gb = place("gb", [P, KC, TB], F32)
        z_hi = place("z_hi", [P, KC, TB], F32R, at_g)
        pw_raw = place("pw_raw", [P, 2, KC, P], F32)
        pw_hi = place("pw_hi", [P, 2, KC, P], F32R)
        pw_lo = place("pw_lo", [P, 2, KC, P], F32R)
        st = place("st", [P, TB], F32)
        sq = place("sq", [P, TB], F32)
        y_sum = place("y_sum", [P, TB], F32)
        q_sum = place("q_sum", [P, TB], F32)
        tok6 = place("tok6", [P, NT, P], F32)
        tok6T = place("tok6T", [P, TB], F32R)
        ln6T = place("ln6T", [P, KC, P], F32R)
        xn = place("xn", [P, D], F32)
        ot = place("ot", [P, NT, 2 * P], F32)
        at_e = top[0]
        ew_raw = place("ew_raw", [P, 3, PW], F32)
        ew_hi = place("ew_hi", [P, 3, PW], F32R)
        ew_lo = place("ew_lo", [P, 3, PW], F32R)
        xg = place("xg", [P, XW], F32)
        gT_hi = place("gT_hi", [P, KC, P], F32R)
        gT_lo = place("gT_lo", [P, KC, P], F32R)
        sh = place("sh", [P, FF], F32)
        hh = place("hh", [P, FF], F32)
        hT_hi = place("hT_hi", [P, FC, P], F32R)
        hT_lo = place("hT_lo", [P, FC, P], F32R)
        ys = place("ys", [P, D], F32)
        end_e = top[0]
        top[0] = at_e
        xt = place("xt", [P, 8, D], F32)
        keys = place("keys", [P, HT // 2], F32)
        key_base = place("key_base", [P, HT // 2], F32)
        key_iota = place("key_iota", [P, HT // 2], I32, top[0] - HT * 4)
        r_raw = place("r_raw", [P, KC, SEL], F32)
        r_hl = place("r_hl", [P, KC, 2 * SEL], F32R)
        lg_lo = place("lg_lo", [P, 2, NT, SEL], F32)
        lg = place("lg", [P, NT, SEL], F32)
        shf = place("shf", [P, NT, SEL], F32)
        ex = place("ex", [P, NT, SEL], F32)
        rep = place("rep", [P, NT, SEL], F32)
        mk = place("mk", [P, NT, 2 * SEL], F32)
        wt = place("wt", [P, 2, NT, SEL], F32)
        m8 = place("m8", [P, NT, 8], F32)
        bn = place("bn", [P, 2, NT, 2, 6], F32)
        mv = place("mv", [P, 2, NT, 2], F32)
        ve = place("ve", [P, NT], F32)
        rs = place("rs", [P, NT], F32)
        sm = place("sm", [P, 2, NT], F32)
        nmr = place("nmr", [P, NT], F32)
        top8 = place("top8", [P, 8], F32)
        ln2 = place("ln2", [P, 2, KC], F32)
        ln2_hi = place("ln2_hi", [P, 2, KC], F32R)
        ln6 = place("ln6", [P, KC, P], F32)
        l1 = place("l1", [P, SLOTS], F32)
        l2 = place("l2", [SEL, 2 * SLOTS], F32)
        lf = place("lf", [SEL, SLOTS], F32)
        ka = place("ka", [P, SEL], I32)
        kb = place("kb", [P, SEL], I32)
        kc = place("kc", [P, SEL], I32)
        assert top[0] <= end_e, (top[0], end_e)

        psX = ctx.enter_context(nc.psum_tensor("psX", [P, 2, TB], F32))
        psH = ctx.enter_context(nc.psum_tensor("psH", [P, 2, TB], F32))
        psY = ctx.enter_context(nc.psum_tensor("psY", [P, 2, TB], F32))
        psA = ctx.enter_context(nc.psum_tensor("psA", [P, 2, TB], F32))
        chunks = lambda ps: ps[:, :, :].rearrange("p a (b c) -> p (a b) c", c=P)

        scratch = nc.dram_tensor("xn_scratch", (NTOK + P, XW), F32).ap()

        s_par = sem("s_par")
        s_const = sem("s_const")
        s_vconst = sem("s_vconst")
        s_lam = sem("s_lam")
        s_rhi, s_rlo = sem("s_rhi"), sem("s_rlo")
        s_xld = [sem(f"s_xld{u}") for u in range(8)]
        s_xst = [sem(f"s_xst{u}") for u in range(8)]
        s_wst = sem("s_wst")
        s_wtf = sem("s_wtf")
        s_spare = sem("s_spare")
        s_x0 = sem("s_x0")
        s_bn = sem("s_bn")
        s_nm = sem("s_nm")
        s_rs = sem("s_rs")
        s_xn = sem("s_xn")
        s_pT = sem("s_pT")
        s_phi, s_plo = sem("s_phi"), sem("s_plo")
        s_rt = sem("s_rt")
        s_lgl = sem("s_lgl")
        s_shf = sem("s_shf")
        s_ex = sem("s_ex")
        s_tk = sem("s_tk")
        s_wm = sem("s_wm")
        s_mT = sem("s_mT")
        s_key = sem("s_key")
        s_ext = sem("s_ext")
        s_l1 = sem("s_l1")
        s_l2 = sem("s_l2")
        s_mrg = sem("s_mrg")
        s_lf = sem("s_lf")
        s_lfT = sem("s_lfT")
        s_ix = sem("s_ix")
        s_pw = [sem(f"s_pw{u}") for u in range(2)]
        s_pwhi, s_pwlo = sem("s_pwhi"), sem("s_pwlo")
        s_pj = sem("s_pj")
        s_vq = sem("s_vq")
        s_go = sem("s_go")
        s_car = sem("s_car")
        s_st0 = sem("s_st0")
        s_sq = sem("s_sq")
        s_sum0 = sem("s_sum0")
        s_sum = sem("s_sum")
        s_smm = sem("s_smm")
        s_col = sem("s_col")
        s_rsy = sem("s_rsy")
        s_tT = sem("s_tT")
        s_t6 = sem("s_t6")
        s_ln = sem("s_ln")
        s_lnT = sem("s_lnT")
        s_l6 = sem("s_l6")
        s_sh = sem("s_sh")
        s_z = sem("s_z")
        s_zhi, s_zlo = sem("s_zhi"), sem("s_zlo")
        s_zlo7 = sem("s_zlo7")
        s_acc = sem("s_acc")
        s_otf = sem("s_otf")
        s_xnl = sem("s_xnl")
        s_xT = sem("s_xT")
        s_xhi, s_xlo = sem("s_xhi"), sem("s_xlo")
        s_ew = [sem(f"s_ew{u}") for u in range(3)]
        s_ewhi, s_ewlo = sem("s_ewhi"), sem("s_ewlo")
        s_ewu = sem("s_ewu")
        s_gi = sem("s_gi")
        s_g = sem("s_g")
        s_w = sem("s_w")
        s_gT = sem("s_gT")
        s_ghi, s_glo = sem("s_ghi"), sem("s_glo")
        s_si = sem("s_si")
        s_hh = sem("s_hh")
        s_hT = sem("s_hT")
        s_hhi, s_hlo = sem("s_hhi"), sem("s_hlo")
        s_ys = sem("s_ys")
        s_sci = sem("s_sci")
        s_sc = sem("s_sc")
        s_ysf = sem("s_ysf")

        s_passed = sem("s_passed")

        N_PAR = 4
        TKS = 7
        CS = 7

        def n1(j, mm, a):
            return NPJ * j + 6 * mm + a

        def half1(j, mm, a):
            return (NPJ // 2) * j + 3 * mm + a // 2

        def n2(j, mm, w):
            return NPJ * j + 3 * KC + 2 * mm + w

        def half2(j, mm):
            return (NPJ // 2) * j + 3 * KC // 2 + mm

        def phases(eng, block):
            block(0, None, False)
            with eng.Fori(1, NB - 1) as j:
                block(j, EPB * (j - 1), False)
            block(NB - 1, EPB * (NB - 2), True)

        def each_qvg(eng, body):
            with eng.Fori(0, KC // 2) as mm:
                body(mm)

        def each_out(eng, first, last, body, between=None):
            if first:
                with eng.Fori(0, 2) as mm:
                    body(mm, True, True, True)
                for i in range(3):
                    between(i)
                    if i < 2:
                        body(2 + i, True, True, False)
            elif last:
                with eng.Fori(0, KC // 2 - 2) as mm:
                    body(mm, True, True, False)
                body(KC // 2 - 2, False, True, False)
                body(KC // 2 - 1, False, False, False)
            else:
                with eng.Fori(0, KC // 2) as mm:
                    body(mm, True, True, False)

        def router_pairs(eng, pair):
            pair(0, True, True)
            if NB // 2 > 2:
                with eng.Fori(1, NB // 2 - 1) as pp:
                    pair(pp, False, True)
            pair(NB // 2 - 1, False, False)

        def row_of(pp, h, s):
            return (NB - 1 - h) * TB + s * P - pp * (2 * TB)

        def wait_alone(eng, semaphore, value):
            eng.wait_ge(semaphore, value)
            eng.sem_inc(s_passed, 1)

        block = ctx.enter_context(nc.Block())

        @block.sync
        def _(sp):
            sp.sem_inc(s_wtf, 2)
            def load_x(row, u):
                sp.dma_start(xt[:, u, :], x[bass.ds(row, P), :]).then_inc(s_xld[u], 16)

            for u in range(NT):
                load_x(row_of(0, 0, u), u)
            sp.dma_start(r_raw[:, :, :], router).then_inc(s_par, 16)
            sp.dma_start(lam[:, :], lam_in).then_inc(s_par, 16)
            sp.dma_start(ln_g[:, :], g_in).then_inc(s_par, 16)
            sp.dma_start(ln_b[:, :], b_in).then_inc(s_par, 16)
            for u in range(NT):
                load_x(row_of(0, 1, u), NT + u)

            def load_proj(slot, row, n_prev=None):
                if n_prev is not None:
                    sp.wait_ge(s_pwlo, n_prev)
                sp.dma_start(pw_raw[:, slot, :, :].rearrange("p k c -> p (k c)"),
                             proj_w[row, :, :]).then_inc(s_pw[slot], 16)

            def copy_x(i):
                sp.dma_start(out[bass.ds(i * P, P), :], x[bass.ds(i * P, P), :]).then_inc(s_x0, 16)

            def store_w(pp, h, first=False):
                if not first:
                    sp.wait_ge(s_wst, 16 * NT * (2 * pp + h))
                    sp.sem_inc(s_wtf, 1)
                wait_alone(sp, s_wm, 2 * pp + h + 1)
                for s in range(NT):
                    sp.dma_start(scratch[bass.ds(row_of(pp, h, s), P), D:XW],
                                 wt[:, h, s, :]).then_inc(s_wst, 16)

            def router_pair(pp, first, more):
                for h in range(2):
                    for s in range(NT):
                        u = NT * h + s
                        wait_alone(sp, s_xn, 8 * pp + u + 1)
                        sp.dma_start(scratch[bass.ds(row_of(pp, h, s), P), 0:D],
                                     xt[:, u, :]).then_inc(s_xst[u], 16)
                    if more:
                        for s in range(NT):
                            u = NT * h + s
                            sp.wait_ge(s_xst[u], 16 * (pp + 1))
                            wait_alone(sp, s_pT, 8 * pp + u + 1)
                            load_x(row_of(pp + 1, h, s), u)
                    if h == 1:
                        store_w(pp, 0, first)
                    elif not first:
                        store_w(pp - 1, 1)
                if first:
                    load_proj(0, 2, 1)
                    load_proj(1, 3, 2)

            def load_piece(e, c, n_prev=None):
                if n_prev is not None:
                    sp.wait_ge(s_ewlo, n_prev)
                sp.dma_start(ew_raw[:, c % 3, :], ew[e, c, :, :]).then_inc(s_ew[c % 3], 16)

            def load_xn(row):
                sp.dma_start(xn[:, :], scratch[bass.ds(row, P), 0:D]).then_inc(s_xnl, 16)

            def load_rest(e):
                for c in range(3):
                    load_piece(e, 3 + c, PIECES * e + 1 + c)

            def load_first(e):
                for c in range(3):
                    load_piece(e, c, PIECES * e - 2 + c)

            load_proj(0, 0)
            load_proj(1, 1)
            router_pairs(sp, router_pair)
            store_w(NB // 2 - 1, 1)
            sp.dma_start(scratch[NTOK:NTOK + P, 0:D], xt[:, 0, :]).then_inc(s_spare, 16)
            sp.dma_start(scratch[NTOK:NTOK + P, D:XW], wt[:, 0, 0, :]).then_inc(s_spare, 16)

            def run(j, e0, last):
                with_e = e0 is not None

                def qvg(mm):
                    per = NTOK // P // (KC // 2)
                    for a in range(2, 8):
                        if with_e and a == 6:
                            load_rest(e0 + mm + 1)
                        load_proj(a % 2, 6 * mm + a + 2, n1(j, mm, a) + 1)
                        if not with_e:
                            for i in range((a - 2) * per // 6, (a - 1) * per // 6):
                                copy_x(per * mm + i)
                    if with_e:
                        load_first(e0 + mm + 2)

                each_qvg(sp, qvg)
                if with_e:
                    load_rest(e0 + 5)
                    load_first(e0 + 6)
                else:
                    sp.wait_ge(s_l1, SLOTS // 8)
                    sp.dma_start(l2[:, SLOTS:2 * SLOTS], l1[SEL:2 * SEL, :]).then_inc(s_l2, 16)
                    for u in range(8):
                        sp.wait_ge(s_xst[u], 16 * (NB // 2))
                    sp.wait_ge(s_spare, 32)
                    load_xn(TB)

                def outp(mm, loads, splits, merge):
                    if not last:
                        sp.wait_ge(s_xT, 4 * j + mm + 1)
                        load_xn((j + 1) * TB + (mm + 1) * P)
                    if with_e:
                        load_rest(e0 + 6 + mm)
                    for w in range(2, 4):
                        if loads:
                            load_proj(w % 2, 3 * KC + 2 * mm + w + 2, n2(j, mm, w) + 1)
                    if with_e and splits:
                        load_first(e0 + 7 + mm)

                def between(i):
                    if i == 0:
                        sp.wait_ge(s_ix, 5)
                        for c in range(3):
                            load_piece(0, c)
                    elif i == 1:
                        load_rest(0)
                    else:
                        load_first(1)

                each_out(sp, not with_e, last, outp, between)

            phases(sp, run)

        @block.gpsimd
        def _(pool):
            pool.sem_inc(s_sum, 1)
            pool.sem_inc(s_otf, 1)
            pool.sem_inc(s_ysf, 1)
            pool.memset(ident[:, :], 0.0).then_inc(s_const, 1)
            pool.wait_ge(s_const, 1)
            pool.affine_select(out=ident[:, :], in_=ident[:, :], compare_op=ALU.not_equal, fill=1.0, base=0,
                               pattern=[[-1, P]], channel_multiplier=1).then_inc(s_const, 1)
            for h in range(2):
                pool.wait_ge(s_const, h + 2)
                pool.iota(key_iota[h * SEL:(h + 1) * SEL, :], pattern=[[-1, HT // 2]],
                          base=HT - h * (HT // 2), channel_multiplier=0).then_inc(s_const, 1)
            pool.wait_ge(s_const, 4)
            pool.wait_ge(s_vconst, 1)
            with pool.Fori(0, NB) as qq:
                pool.wait_ge(s_bn, 3 * qq + 3)
                pool.tensor_tensor(rs[:, :], ve[:, :], half[:, 0:NT], ALU.pow).then_inc(s_rs, 1)

            def gather(e):
                pool.tensor_copy(g_idx[:, :], idx[:, bass.ds(e, 1)]).then_inc(s_gi, 1)
                wait_alone(pool, s_gi, e + 1)
                pool.indirect_dma_start(xg[:, :], None, scratch,
                                        bass.IndirectOffsetOnAxis(ap=g_idx[:, 0:1], axis=0)
                                        ).then_inc(s_g, 16)

            def gather_next(e):
                pool.wait_ge(s_gT, e + 1)
                pool.wait_ge(s_w, e + 1)
                gather(e + 1)

            def scatter(e):
                pool.tensor_copy(s_idx[:, :], idx[:, bass.ds(e, 1)]).then_inc(s_sci, 1)
                pool.wait_ge(s_sci, e + 1)
                wait_alone(pool, s_ys, e + 1)
                pool.indirect_dma_start(out, bass.IndirectOffsetOnAxis(ap=s_idx[:, 0:1], axis=0),
                                        ys[:, :], None, compute_op=ALU.add).then_inc(s_sc, 16)
                pool.wait_ge(s_sc, 16 * (e + 1))
                pool.sem_inc(s_ysf, 1)

            def add_sums(j, mm, h):
                i = KC * j + 2 * mm + h
                pool.wait_ge(s_sq, i + 1)
                pool.wait_ge(s_sum, i + 1)
                pool.tensor_tensor(y_sum[:, :], y_sum[:, :], yb[:, 2 * mm + h, :], ALU.add)
                pool.tensor_tensor(q_sum[:, :], q_sum[:, :], sq[:, :], ALU.add).then_inc(s_sum, 1)

            def run(j, e0, last):
                with_e = e0 is not None
                if with_e:
                    wait_alone(pool, s_smm, j)
                pool.memset(y_sum[:, :], 0.0)
                pool.memset(q_sum[:, :], 0.0).then_inc(s_sum0, 1)
                wait_alone(pool, s_sum0, j + 1)

                def qvg(mm):
                    add_sums(j, mm, 0)
                    if with_e:
                        scatter(e0 + mm)
                    add_sums(j, mm, 1)
                    if with_e:
                        gather_next(e0 + mm + 1)

                each_qvg(pool, qvg)
                pool.wait_ge(s_col, CS * j + 4)
                pool.tensor_tensor(col[:, 4, :], col[:, 3, :], half[:, 0:NT], ALU.pow).then_inc(s_rsy, 1)
                if with_e:
                    e = e0 + 5
                    pool.wait_ge(s_ewhi, PIECES * e + 2)
                    pool.wait_ge(s_ewlo, PIECES * e + 1)
                    pool.tensor_tensor(ew_lo[:, 1, :], ew_raw[:, 1, :], ew_hi[:, 1, :].bitcast(F32),
                                       ALU.subtract).then_inc(s_ewlo, 1)
                for m in range(KC - 1):
                    pool.wait_ge(s_zhi, KC * j + m + 1)
                    pool.tensor_tensor(z_lo[:, m, :], yb[:, m, :], z_hi[:, m, :].bitcast(F32),
                                       ALU.subtract).then_inc(s_zlo, 1)
                if with_e:
                    gather_next(e0 + 5)
                    scatter(e0 + 4)
                if not with_e:
                    pool.wait_ge(s_x0, 16 * (NTOK // P))

                def outp(mm, loads, splits, merge):
                    if with_e:
                        scatter(e0 + 5 + mm)
                    pool.wait_ge(s_go, 16 * j + 8 + 2 * mm + 2 + 2)
                    pool.dma_start(out[bass.ds(j * TB, TB), bass.ds(mm * 2 * P, 2 * P)]
                                   .rearrange("(t p) c -> p t c", p=P), ot[:, :, :],
                                   accum_op=ALU.add).then_inc(s_acc, 16)
                    pool.wait_ge(s_acc, 16 * (4 * j + mm + 1))
                    pool.sem_inc(s_otf, 1)
                    if with_e and splits:
                        gather_next(e0 + 6 + mm)

                def between(i):
                    if i == 0:
                        pool.wait_ge(s_ix, 5)
                        pool.wait_ge(s_wst, 16 * NB * NT)
                        for u in range(8):
                            pool.wait_ge(s_xst[u], 16 * (NB // 2))
                        pool.wait_ge(s_spare, 32)
                        gather(0)
                    elif i == 2:
                        gather_next(0)

                each_out(pool, not with_e, last, outp, between)

            phases(pool, run)
            scatter(experts - 1)

        @block.scalar
        def _(act):
            act.sem_inc(s_go, 2)
            act.wait_ge(s_par, 16 * N_PAR)
            act.activation(lam[:, :], lam[:, :], ACT.Sigmoid).then_inc(s_lam, 1)
            act.activation(r_hl[:, :, 0:SEL], r_raw[:, :, :], ACT.Copy).then_inc(s_rhi, 1)

            def normalize(pp, h, s):
                if s == 0:
                    act.wait_ge(s_nm, 2 * pp + h + 1)
                u = NT * h + s
                act.activation(xt[:, u, :], xt[:, u, :], ACT.Identity, bias=nmr[:, s:s + 1],
                               scale=rs[:, s:s + 1]).then_inc(s_xn, 1)

            def exp_of(pp, h):
                act.wait_ge(s_shf, 2 * pp + h + 1)
                act.activation(ex[:, :, :], shf[:, :, :], ACT.Exp).then_inc(s_ex, 1)

            def logits_lo(pp, h):
                act.wait_ge(s_rt, 2 * pp + h + 1)
                act.activation(lg_lo[:, h, :, :], psA[:, h, :].rearrange("p (s e) -> p s e", e=2 * SEL)
                               [:, :, SEL:2 * SEL], ACT.Copy).then_inc(s_lgl, 1)

            def router_pair(pp, first, more):
                for h in range(2):
                    q = 2 * pp + h

                    def hi(s):
                        act.wait_ge(s_pT, NT * q + s + 1)
                        act.activation((z_hi, xT_hi)[h][:, :, s * P:(s + 1) * P], chunks((psX, psH)[s % 2]),
                                       ACT.Copy).then_inc(s_phi, 1)

                    normalize(pp, h, 0)
                    normalize(pp, h, 1)
                    if not first:
                        exp_of(pp - 1, h)
                    hi(0)
                    for s in range(2, NT):
                        normalize(pp, h, s)
                        hi(s - 1)
                    hi(NT - 1)
                    if h == 1:
                        logits_lo(pp, 0)
                    elif not first:
                        logits_lo(pp - 1, 1)
                if first:
                    for n in range(2):
                        proj_hi(n, n, 0, None)

            def proj_hi(n, slot, hf, used):
                act.wait_ge(s_pw[slot], 16 * (hf + 1))
                if used is not None:
                    act.wait_ge(s_pj, used)
                act.activation(pw_hi[:, slot, :, :], pw_raw[:, slot, :, :], ACT.Copy).then_inc(s_pwhi, 1)

            def piece_hi(e, c, used=True):
                act.wait_ge(s_ew[c % 3], 16 * (2 * e + c // 3 + 1))
                if used:
                    act.wait_ge(s_ewu, PIECES * e + c - 2)
                act.activation(ew_hi[:, c % 3, :], ew_raw[:, c % 3, :], ACT.Copy).then_inc(s_ewhi, 1)

            def silu_h(e):
                act.wait_ge(s_ewu, PIECES * e + 4)
                act.activation(sh[:, :], psH[:, 0, 0:FF], ACT.Silu).then_inc(s_si, 1)

            def hT_hi_of(e):
                act.wait_ge(s_hT, e + 1)
                act.activation(hT_hi[:, :, :].rearrange("p f c -> p (f c)"), psX[:, 0, 0:FF],
                               ACT.Copy).then_inc(s_hhi, 1)

            def y_out(e, part=None):
                if part != 1:
                    act.wait_ge(s_w, e + 1)
                    act.wait_ge(s_ysf, e + 1)
                for h in range(2) if part is None else (part,):
                    wait_alone(act, s_ewu, PIECES * e + 5 + h)
                    o = act.activation(ys[:, h * TB:(h + 1) * TB], psY[:, h, :], ACT.Copy,
                                       scale=w_tab[:, bass.ds(e, 1)])
                if part != 0:
                    o.then_inc(s_ys, 1)

            def gT_hi_of(e):
                wait_alone(act, s_g, 16 * (e + 1))
                act.activation(w_tab[:, bass.ds(e, 1)], xg[:, bass.ds(e + D, 1)], ACT.Copy).then_inc(s_w, 1)
                act.wait_ge(s_gT, e + 1)
                act.activation(gT_hi[:, :, :], chunks(psX), ACT.Copy).then_inc(s_ghi, 1)

            def hidden_part(e, c0=3):
                for c in range(c0, PIECES):
                    piece_hi(e, c)
                silu_h(e)

            def square(j, mm, h):
                act.wait_ge(s_vq, 16 * j + 4 * mm + 2 * h + 3)
                act.wait_ge(s_sum, KC * j + 2 * mm + h + 1)
                act.activation(sq[:, :], yb[:, 2 * mm + h, :], ACT.Square).then_inc(s_sq, 1)

            def gate(j, mm, h):
                act.wait_ge(s_pj, n1(j, mm, 3 * h + 2) + 1)
                act.activation(gb[:, 2 * mm + h, :], psA[:, h, :], ACT.Silu).then_inc(s_go, 1)

            def rows6(j):
                act.wait_ge(s_tT, j + 1)
                act.activation(tok6T[:, :], psA[:, 1, :], ACT.Copy).then_inc(s_t6, 1)

            def z_his(j, i):
                for m in (2 * i, 2 * i + 1):
                    act.wait_ge(s_z, 2 * KC * j + 4 * i + 3 + m % 2)
                    act.activation(z_hi[:, m, :], yb[:, m, :], ACT.Copy).then_inc(s_zhi, 1)

            def out_copy(j, mm, w):
                act.wait_ge(s_pj, n2(j, mm, w) + 1)
                if w == 0:
                    act.wait_ge(s_otf, 4 * j + mm + 1)
                for t in (2 * w, 2 * w + 1):
                    o = act.activation(ot[:, t, :], psA[:, w, (t % 2) * 2 * P:(t % 2 + 1) * 2 * P], ACT.Copy,
                                       scale=col[:, 4, t:t + 1])
                o.then_inc(s_go, 1)

            router_pairs(act, router_pair)
            exp_of(NB // 2 - 1, 0)
            logits_lo(NB // 2 - 1, 1)
            act.wait_ge(s_lnT, 1)
            act.activation(ln6T[:, :, :], chunks(psX), ACT.Copy).then_inc(s_l6, 1)
            exp_of(NB // 2 - 1, 1)

            def run(j, e0, last):
                with_e = e0 is not None

                def qvg(mm):
                    e = None if not with_e else e0 + mm
                    S = lambda a: proj_hi(None, a % 2, half1(j, mm, a), n1(j, mm, a) - 1)
                    S(2)
                    S(3)
                    if with_e:
                        hT_hi_of(e)
                        piece_hi(e + 1, 0)
                    square(j, mm, 0)
                    gate(j, mm, 0)
                    S(4)
                    if with_e:
                        y_out(e)
                        piece_hi(e + 1, 1)
                        piece_hi(e + 1, 2)
                        gT_hi_of(e + 1)
                    S(5)
                    S(6)
                    square(j, mm, 1)
                    gate(j, mm, 1)
                    S(7)
                    if with_e:
                        hidden_part(e + 1)

                each_qvg(act, qvg)
                if with_e:
                    e = e0 + 4
                    hT_hi_of(e)
                    piece_hi(e + 1, 0)
                rows6(j)
                if with_e:
                    gT_hi_of(e + 1)
                    y_out(e, 0)
                    piece_hi(e + 1, 1)
                    y_out(e, 1)
                z_his(j, 0)
                if with_e:
                    piece_hi(e + 1, 2)
                z_his(j, 1)
                if with_e:
                    piece_hi(e + 1, 3)
                z_his(j, 2)
                z_his(j, 3)
                if with_e:
                    silu_h(e + 1)
                    piece_hi(e + 1, 4)
                    piece_hi(e + 1, 5)

                def outp(mm, loads, splits, merge):
                    e = None if not with_e else e0 + 5 + mm
                    if with_e:
                        hT_hi_of(e)
                    if not last:
                        act.wait_ge(s_xT, 4 * j + mm + 1)
                        act.activation(xT_hi[:, :, bass.ds(mm * P, P)], chunks(psH), ACT.Copy).then_inc(s_xhi, 1)
                    if with_e:
                        piece_hi(e + 1, 0)
                    out_copy(j, mm, 0)
                    if with_e:
                        y_out(e, 0)
                        piece_hi(e + 1, 1)
                        y_out(e, 1)
                        gT_hi_of(e + 1)
                        piece_hi(e + 1, 2)
                    if splits:
                        proj_hi(None, 0, half2(j, mm + 1), n2(j, mm, 1) + 1)
                        proj_hi(None, 1, half2(j, mm + 1), n2(j, mm, 1) + 1)
                    if with_e:
                        piece_hi(e + 1, 3)
                    out_copy(j, mm, 1)
                    if with_e:
                        hidden_part(e + 1, c0=4)

                def between(i):
                    if i == 1:
                        gT_hi_of(0)
                        for c in range(3):
                            piece_hi(0, c, used=False)
                    elif i == 2:
                        hidden_part(0)

                each_out(act, not with_e, last, outp, between)

            phases(act, run)
            hT_hi_of(experts - 1)
            y_out(experts - 1)

        @block.vector
        def _(dve):
            dve.sem_inc(s_vq, 1)
            dve.memset(half[:, :], -0.5).then_inc(s_vconst, 1)

            def stats_tile(pp, h, s):
                dve.wait_ge(s_xld[NT * h + s], 16 * (pp + 1))
                for i in range(2):
                    o = dve.bn_stats(bn[:, h, s, i, :], xt[:, NT * h + s, i * TB:(i + 1) * TB])
                if s == NT - 1:
                    o.then_inc(s_bn, 1)

            def stats_of(pp, h):
                q = 2 * pp + h
                wait_alone(dve, s_bn, 3 * q + 1)
                for s in range(NT):
                    o = dve.bn_aggr(mv[:, h, s, :], bn[:, h, s, :, :].rearrange("p a b -> p (a b)"))
                o.then_inc(s_bn, 1)
                dve.wait_ge(s_bn, 3 * q + 2)
                dve.tensor_scalar(ve[:, :], mv[:, h, :, 1], EPS, None, ALU.add).then_inc(s_bn, 1)

            def shift_of(pp, h):
                dve.wait_ge(s_rs, 2 * pp + h + 1)
                dve.scalar_tensor_tensor(nmr[:, :], mv[:, h, :, 0], -1.0, rs[:, :], ALU.mult,
                                         ALU.mult).then_inc(s_nm, 1)

            def low(pp, h, s):
                dst, hi = ((z_lo, z_hi), (xT_lo, xT_hi))[h]
                dve.wait_ge(s_phi, NT * (2 * pp + h) + s + 1)
                c = slice(s * P, (s + 1) * P)
                dve.tensor_tensor(dst[:, :, c], chunks((psX, psH)[s % 2]), hi[:, :, c].bitcast(F32),
                                  ALU.subtract).then_inc(s_plo, 1)

            def take_logits(pp, h):
                dve.wait_ge(s_lgl, 2 * pp + h + 1)
                dve.tensor_tensor(lg[:, :, :], psA[:, h, :].rearrange("p (s e) -> p s e", e=2 * SEL)
                                  [:, :, 0:SEL], lg_lo[:, h, :, :], ALU.add).then_inc(s_tk, 1)

            def top8_of(pp, h):
                q = 2 * pp + h
                E = experts
                own = lambda i: dve.wait_ge(s_tk, TKS * q + i)
                wait_alone(dve, s_tk, TKS * q + 1)
                for s in range(NT):
                    o = dve.max(m8[:, s, :], lg[:, s, 0:E])
                o.then_inc(s_tk, 1)
                own(2)
                dve.tensor_tensor(shf[:, :, :], lg[:, :, :], m8[:, :, 0:1].to_broadcast([P, NT, SEL]),
                                  ALU.subtract).then_inc(s_shf, 1)
                for s in range(NT):
                    o = dve.match_replace(rep[:, s, 0:E], m8[:, s, :], lg[:, s, 0:E], NEG)
                o.then_inc(s_tk, 1)
                own(3)
                m = mk[:, :, (1 - h) * SEL:(1 - h) * SEL + E]
                dve.tensor_scalar(m, rep[:, :, 0:E], NEG, None, ALU.is_equal).then_inc(s_tk, 1)
                own(4)
                dve.wait_ge(s_ex, q + 1)
                w = wt[:, h, :, 0:E]
                dve.wait_ge(s_wtf, q + 1)
                dve.tensor_tensor(w, ex[:, :, 0:E], m, ALU.mult).then_inc(s_tk, 1)
                own(5)
                dve.tensor_reduce(sm[:, 0, :], w, AX_X, ALU.add).then_inc(s_tk, 1)
                own(6)
                dve.reciprocal(sm[:, 1, :], sm[:, 0, :]).then_inc(s_tk, 1)
                own(7)
                dve.tensor_tensor(w, w, sm[:, 1, :].unsqueeze(2).to_broadcast([P, NT, E]),
                                  ALU.mult).then_inc(s_wm, 1)

            def keys_of(pp):
                wait_alone(dve, s_mT, pp + 1)
                b = batches - 1 - pp
                view = lambda t: t[:, :].rearrange("p (s b) -> p s b", b=batches)[:, :, bass.ds(b, 1)]
                dve.scalar_tensor_tensor(view(keys), psY[:, 0, :].unsqueeze(2), float(HT), view(key_base),
                                         ALU.mult, ALU.add).then_inc(s_key, 1)

            def router_pair(pp, first, more):
                for h in range(2):
                    nxt = h == 0 or more
                    for s in range(NT):
                        low(pp, h, s)
                        if nxt:
                            stats_tile(pp + h, 1 - h, s)
                    if nxt:
                        stats_of(pp + h, 1 - h)
                    prev = (pp, 0) if h == 1 else None if first else (pp - 1, 1)
                    if h == 1 and not first:
                        keys_of(pp - 1)
                    if prev:
                        take_logits(*prev)
                    if nxt:
                        shift_of(pp + h, 1 - h)
                    if prev:
                        top8_of(*prev)
                if first:
                    for n in range(2):
                        proj_lo(n, n)
                    dve.wait_ge(s_const, 4)
                    dve.tensor_copy(key_base[:, :], key_iota[:, :]).then_inc(s_vconst, 1)
                    dve.wait_ge(s_vconst, 3)

            def find8(src, into, n, steps, copied):
                dve.max(top8[0:src.shape[0], :], src).then_inc(steps, 1)
                dve.wait_ge(steps, 2 * n + 1)
                dve.tensor_copy(into[:, bass.ds(n * 8, 8)], top8[0:src.shape[0], :]).then_inc(copied, 1)

            def strike8(src, n, steps):
                dve.match_replace(src, top8[0:src.shape[0], :], src, -1.0).then_inc(steps, 1)
                wait_alone(dve, steps, 2 * n + 2)

            def proj_lo(n, slot):
                dve.wait_ge(s_pwhi, n + 1)
                dve.tensor_tensor(pw_lo[:, slot, :, :], pw_raw[:, slot, :, :], pw_hi[:, slot, :, :].bitcast(F32),
                                  ALU.subtract).then_inc(s_pwlo, 1)

            def piece_lo(e, c):
                dve.wait_ge(s_ewhi, PIECES * e + c + 1)
                dve.tensor_tensor(ew_lo[:, c % 3, :], ew_raw[:, c % 3, :], ew_hi[:, c % 3, :].bitcast(F32),
                                  ALU.subtract).then_inc(s_ewlo, 1)

            def hidden(e):
                dve.wait_ge(s_si, e + 1)
                dve.tensor_tensor(hh[:, :], psH[:, 1, 0:FF], sh[:, :], ALU.mult).then_inc(s_hh, 1)

            def hidden_part(e, c0=3):
                for c in range(c0, PIECES):
                    piece_lo(e, c)
                hidden(e)

            def hT_lo_of(e):
                dve.wait_ge(s_hhi, e + 1)
                dve.tensor_tensor(hT_lo[:, :, :].rearrange("p f c -> p (f c)"), psX[:, 0, 0:FF],
                                  hT_hi[:, :, :].rearrange("p f c -> p (f c)").bitcast(F32),
                                  ALU.subtract).then_inc(s_hlo, 1)

            def gT_lo_of(e):
                dve.wait_ge(s_ghi, e + 1)
                dve.tensor_tensor(gT_lo[:, :, :], chunks(psX), gT_hi[:, :, :].bitcast(F32),
                                  ALU.subtract).then_inc(s_glo, 1)

            def scan(j, mm, h):
                m = 2 * mm + h
                dve.wait_ge(s_pj, n1(j, mm, 3 * h) + 1)
                dve.tensor_tensor_scan(st[:, :], lam[:, bass.ds(m, 1)].to_broadcast([P, TB]), psA[:, h, :],
                                       start[:, bass.ds(m, 1)], ALU.mult, ALU.add).then_inc(s_vq, 1)

            def times_q(j, mm, h):
                m = 2 * mm + h
                dve.wait_ge(s_pj, n1(j, mm, 3 * h + 1) + 1)
                dve.wait_ge(s_vq, 16 * j + 4 * mm + 2 * h + 2)
                dve.tensor_tensor(yb[:, m, :], psA[:, 1 - h, :], st[:, :], ALU.mult).then_inc(s_vq, 1)
                dve.tensor_copy(carry[:, bass.ds(m, 1)], st[:, TB - 1:TB]).then_inc(s_car, 1)

            def z_of(j, i):
                pair = (2 * i, 2 * i + 1)
                for m in pair:
                    dve.wait_ge(s_sh, KC * j + m + 1)
                    dve.scalar_tensor_tensor(yb[:, m, :], yb[:, m, :], ln_g[:, m:m + 1], psA[:, m % 2, :],
                                             ALU.mult, ALU.add).then_inc(s_z, 1)
                for m in pair:
                    dve.wait_ge(s_z, 2 * KC * j + 4 * i + 1 + m % 2)
                    dve.tensor_tensor(yb[:, m, :], yb[:, m, :], gb[:, m, :], ALU.mult).then_inc(s_z, 1)

            def token_var(j):
                own = lambda i: dve.wait_ge(s_col, CS * j + i)
                dve.wait_ge(s_smm, j + 1)
                dve.tensor_scalar(col[:, 0:2, :], psA[:, 0, 0:2 * NT].rearrange("p (i t) -> p i t", t=NT),
                                  RN, None, ALU.mult).then_inc(s_col, 1)
                own(1)
                dve.tensor_tensor(col[:, 2, :], col[:, 0, :], col[:, 0, :], ALU.mult).then_inc(s_col, 1)
                own(2)
                dve.tensor_tensor(col[:, 2, :], col[:, 1, :], col[:, 2, :], ALU.subtract).then_inc(s_col, 1)
                own(3)
                dve.tensor_scalar(col[:, 3, :], col[:, 2, :], 0.0, EPS, ALU.max, ALU.add).then_inc(s_col, 1)

            def token_six(j):
                own = lambda i: dve.wait_ge(s_col, CS * j + i)
                dve.wait_ge(s_rsy, j + 1)
                dve.tensor_tensor(col[:, 1, :], col[:, 3, :], col[:, 4, :], ALU.mult).then_inc(s_col, 1)
                own(5)
                dve.tensor_copy(col_hi[:, :, :], col[:, 0:2, :]).then_inc(s_col, 1)
                own(6)
                six = tok6[:, :, 0:6].rearrange("p t (i r) -> p i t r", r=3)
                hi = col_hi[:, :, :].bitcast(F32)
                for r in range(2):
                    dve.tensor_copy(six[:, :, :, r], hi)
                dve.tensor_tensor(six[:, :, :, 2], col[:, 0:2, :], hi, ALU.subtract).then_inc(s_col, 1)

            for s in range(NT):
                stats_tile(0, 0, s)
            stats_of(0, 0)
            shift_of(0, 0)
            dve.memset(carry[:, :], 0.0).then_inc(s_car, 1)
            dve.memset(idx[:, :], 0)
            dve.memset(ones[:, :], 1.0)
            dve.memset(wt[:, :, :, :], 0.0)
            for b in range(NB):
                dve.memset(keep[:, b:b + 1], float(b % 2))
            dve.memset(mk[:, :, :], 0.0)
            dve.memset(tok6[:, :, :], 0.0)
            dve.memset(ln6[:, :, :], 0.0).then_inc(s_vconst, 1)
            dve.wait_ge(s_vconst, 2)
            dve.wait_ge(s_par, 16 * N_PAR)
            dve.tensor_scalar(ln2[:, 0, :], ln_g[:, :], -1.0, None, ALU.mult)
            dve.tensor_copy(ln2[:, 1, :], ln_b[:, :]).then_inc(s_ln, 1)
            dve.wait_ge(s_ln, 1)
            dve.tensor_copy(ln2_hi[:, :, :], ln2[:, :, :]).then_inc(s_ln, 1)
            dve.wait_ge(s_ln, 2)
            six = ln6[:, :, 0:6].rearrange("p k (i r) -> p i k r", r=3)
            hi = ln2_hi[:, :, :].bitcast(F32)
            for r in (0, 2):
                dve.tensor_copy(six[:, :, :, r], hi)
            dve.tensor_tensor(six[:, :, :, 1], ln2[:, :, :], hi, ALU.subtract).then_inc(s_ln, 1)
            dve.wait_ge(s_rhi, 1)
            dve.tensor_tensor(r_hl[:, :, SEL:2 * SEL], r_raw[:, :, :], r_hl[:, :, 0:SEL].bitcast(F32),
                              ALU.subtract).then_inc(s_rlo, 1)
            router_pairs(dve, router_pair)
            take_logits(NB // 2 - 1, 1)
            top8_of(NB // 2 - 1, 1)
            keys_of(NB // 2 - 1)

            def run(j, e0, last):
                with_e = e0 is not None
                dve.wait_ge(s_car, KC * j + 1)
                dve.tensor_scalar(start[:, :], carry[:, :], keep[:, bass.ds(j, 1)], None,
                                  ALU.mult).then_inc(s_st0, 1)
                wait_alone(dve, s_st0, j + 1)
                if not with_e:
                    dve.wait_ge(s_key, NB // 2)
                    dve.wait_ge(s_lam, 1)

                def qvg(mm):
                    e = None if not with_e else e0 + mm
                    S = lambda a: proj_lo(n1(j, mm, a), a % 2)

                    def find(r):
                        if not with_e:
                            find8(keys[:, :], l1, 4 * mm + r, s_ext, s_l1)

                    def strike(r):
                        if not with_e:
                            strike8(keys[:, :], 4 * mm + r, s_ext)

                    scan(j, mm, 0)
                    S(2)
                    find(0)
                    times_q(j, mm, 0)
                    S(3)
                    strike(0)
                    if with_e:
                        hT_lo_of(e)
                        piece_lo(e + 1, 0)
                    S(4)
                    if with_e:
                        piece_lo(e + 1, 1)
                        piece_lo(e + 1, 2)
                        gT_lo_of(e + 1)
                    find(1)
                    strike(1)
                    scan(j, mm, 1)
                    S(5)
                    find(2)
                    times_q(j, mm, 1)
                    S(6)
                    strike(2)
                    S(7)
                    find(3)
                    strike(3)
                    if with_e:
                        hidden_part(e + 1)

                each_qvg(dve, qvg)
                token_var(j)
                if with_e:
                    e = e0 + 4
                    hT_lo_of(e)
                token_six(j)
                if not with_e:
                    dve.wait_ge(s_l1, SLOTS // 8)
                    dve.tensor_copy(l2[:, 0:SLOTS], l1[0:SEL, :]).then_inc(s_lf, 1)
                if with_e:
                    piece_lo(e + 1, 0)
                z_of(j, 0)
                if with_e:
                    gT_lo_of(e + 1)
                z_of(j, 1)
                if with_e:
                    dve.wait_ge(s_ewlo, PIECES * (e + 1) + 2)
                    piece_lo(e + 1, 2)
                z_of(j, 2)
                if with_e:
                    piece_lo(e + 1, 3)
                z_of(j, 3)
                dve.wait_ge(s_zhi, KC * (j + 1))
                dve.tensor_tensor(z_lo[:, KC - 1, :], yb[:, KC - 1, :], z_hi[:, KC - 1, :].bitcast(F32),
                                  ALU.subtract).then_inc(s_zlo7, 1)
                if with_e:
                    hidden(e + 1)
                    piece_lo(e + 1, 4)
                    piece_lo(e + 1, 5)
                if not with_e:
                    dve.wait_ge(s_l2, 16)
                    dve.wait_ge(s_lf, 1)

                def outp(mm, loads, splits, merge):
                    if with_e:
                        e = e0 + 5 + mm
                        hT_lo_of(e)
                    for r in range(8 if merge else 0):
                        find8(l2[:, :], lf, 8 * mm + r, s_mrg, s_lf)
                        strike8(l2[:, :], 8 * mm + r, s_mrg)
                    if not last:
                        dve.wait_ge(s_xhi, 4 * j + mm + 1)
                        c = bass.ds(mm * P, P)
                        dve.tensor_tensor(xT_lo[:, :, c], chunks(psH), xT_hi[:, :, c].bitcast(F32),
                                          ALU.subtract).then_inc(s_xlo, 1)
                    if with_e:
                        piece_lo(e + 1, 0)
                        piece_lo(e + 1, 1)
                        gT_lo_of(e + 1)
                        piece_lo(e + 1, 2)
                    if splits:
                        proj_lo(n2(j, mm, 2), 0)
                        proj_lo(n2(j, mm, 3), 1)
                    if with_e:
                        hidden_part(e + 1)

                def indices():
                    own = lambda i: dve.wait_ge(s_ix, i)
                    dve.wait_ge(s_lfT, 1)
                    dve.tensor_scalar(ka[:, :], psX[:, 0, 0:SEL], -1.0, float(2 * HT), ALU.mult,
                                      ALU.add).then_inc(s_ix, 1)
                    own(1)
                    dve.tensor_scalar(kb[:, :], ka[:, :], batches - 1, seq.bit_length() - 1, ALU.bitwise_and,
                                      ALU.logical_shift_left).then_inc(s_ix, 1)
                    own(2)
                    dve.tensor_scalar(kc[:, :], ka[:, :], HT - 1, batches.bit_length() - 1, ALU.bitwise_and,
                                      ALU.logical_shift_right).then_inc(s_ix, 1)
                    own(3)
                    dve.tensor_tensor(idx[:, 0:experts], kb[:, 0:experts], kc[:, 0:experts],
                                      ALU.add).then_inc(s_ix, 2)

                def between(i):
                    if i == 0:
                        indices()
                    elif i == 1:
                        gT_lo_of(0)
                        for c in range(3):
                            piece_lo(0, c)
                    else:
                        hidden_part(0)

                each_out(dve, not with_e, last, outp, between)

            phases(dve, run)
            hT_lo_of(experts - 1)

        @block.tensor
        def _(pe):
            def three(dst, l_hi, l_lo, r_hi_, r_lo_, first, last):
                pe.matmul(dst, l_hi, r_hi_, start=first, stop=False)
                pe.matmul(dst, l_hi, r_lo_, start=False, stop=False)
                return pe.matmul(dst, l_lo, r_hi_, start=False, stop=last)

            pe.wait_ge(s_const, 2)

            def turn_tile(pp, h, s):
                q = 2 * pp + h
                pe.wait_ge(s_xn, NT * q + s + 1)
                if s >= 2:
                    pe.wait_ge(s_plo, NT * q + s - 1)
                for k in range(KC):
                    o = pe.transpose((psX, psH)[s % 2][:, k // 4, (k % 4) * P:(k % 4 + 1) * P],
                                     xt[:, NT * h + s, k * P:(k + 1) * P], ident[:, :])
                o.then_inc(s_pT, 1)

            def logits(pp, h, s):
                q = 2 * pp + h
                pe.wait_ge(s_plo, NT * q + s + 1)
                c = slice(s * P, (s + 1) * P)
                for k in range(KC):
                    for i, t in enumerate(((z_hi, z_lo), (xT_hi, xT_lo))[h]):
                        o = pe.matmul(psA[:, h, s * 2 * SEL:(s + 1) * 2 * SEL], t[:, k, c], r_hl[:, k, :],
                                      start=k == 0 and i == 0, stop=k == KC - 1 and i == 1)
                if s == NT - 1:
                    o.then_inc(s_rt, 1)

            def masks_turn(pp):
                pe.wait_ge(s_tk, TKS * (2 * pp + 1) + 4)
                for s in range(NT):
                    o = pe.transpose(psY[:, 0, s * P:(s + 1) * P], mk[:, s, :], ident[:, :])
                o.then_inc(s_mT, 1)

            def router_pair(pp, first, more):
                for h in range(2):
                    prev = (pp, 0) if h == 1 else None if first else (pp - 1, 1)
                    if first and h == 1:
                        pe.wait_ge(s_rlo, 1)
                    turn_tile(pp, h, 0)
                    turn_tile(pp, h, 1)
                    if prev:
                        logits(*prev, 0)
                        logits(*prev, 1)
                    turn_tile(pp, h, 2)
                    turn_tile(pp, h, 3)
                    if prev:
                        logits(*prev, 2)
                        logits(*prev, 3)
                    if h == 1 and not first:
                        masks_turn(pp - 1)

            router_pairs(pe, router_pair)
            for s in range(NT):
                logits(NB // 2 - 1, 1, s)
            pe.wait_ge(s_ln, 3)
            for k in range(KC):
                o = pe.transpose(psX[:, k // 4, (k % 4) * P:(k % 4 + 1) * P], ln6[:, k, :], ident[:, :])
            o.then_inc(s_lnT, 1)
            masks_turn(NB // 2 - 1)

            def proj(n, bank, slot, hi, lo):
                pe.wait_ge(s_pwlo, n + 1)
                for k in range(KC):
                    o = three(psA[:, bank, :], pw_hi[:, slot, k, :], pw_lo[:, slot, k, :], hi[:, k, :],
                              lo[:, k, :], k == 0, k == KC - 1)
                o.then_inc(s_pj, 1)

            def qvg_proj(j, mm, a):
                vq = {0: 0, 2: 1, 3: 2, 5: 3}
                go = {0: -1, 1: 0, 4: 1}
                if a in vq:
                    pe.wait_ge(s_vq, 16 * j + 4 * mm + vq[a] + 1)
                if a in go:
                    pe.wait_ge(s_go, 16 * j + 2 * mm + go[a] + 2)
                proj(n1(j, mm, a), a % 2, a % 2, xT_hi, xT_lo)

            def out_proj(j, mm, w, tiles=(0, 1)):
                if w == 0:
                    pe.wait_ge(s_go, 16 * j + 7 + 2 * mm + 2)
                    pe.wait_ge(s_z, 2 * KC * j + 2 * KC - 3)
                    pe.wait_ge(s_zlo, (KC - 1) * j + KC - 2)
                    pe.wait_ge(s_pwlo, n2(j, mm, 1) + 1)
                elif 0 in tiles:
                    pe.wait_ge(s_go, 16 * j + 8 + 2 * mm + 2)
                for t in tiles:
                    c = slice((2 * w + t) * P, (2 * w + t + 1) * P)
                    for k in range(KC):
                        if w == 0 and t == 0 and k == KC - 2:
                            pe.wait_ge(s_zlo, (KC - 1) * (j + 1))
                        if w == 0 and t == 0 and k == KC - 1:
                            pe.wait_ge(s_zlo7, j + 1)
                        o = three(psA[:, w, t * 2 * P:(t + 1) * 2 * P], z_hi[:, k, c], z_lo[:, k, c],
                                  pw_hi[:, :, k, :], pw_lo[:, :, k, :], k == 0, k == KC - 1)
                if 1 in tiles:
                    o.then_inc(s_pj, 1)

            def gather_turn(e):
                pe.wait_ge(s_g, 16 * (e + 1))
                for k in range(KC):
                    o = pe.transpose(psX[:, k // 4, (k % 4) * P:(k % 4 + 1) * P], xg[:, k * P:(k + 1) * P],
                                     ident[:, :])
                o.then_inc(s_gT, 1)

            def hidden_mm(e, parts=range(4)):
                for c in parts:
                    if c == 0:
                        pe.wait_ge(s_glo, e + 1)
                    pe.wait_ge(s_ewlo, PIECES * e + c + 1)
                    for kk in range(PK):
                        k = PK * c + kk
                        for w in range(2):
                            cols = slice((2 * kk + w) * FF, (2 * kk + w + 1) * FF)
                            o = three(psH[:, w, 0:FF], gT_hi[:, k, :], gT_lo[:, k, :], ew_hi[:, c % 3, cols],
                                      ew_lo[:, c % 3, cols], k == 0, k == KC - 1)
                    o.then_inc(s_ewu, 1)

            def hidden_turn(e):
                pe.wait_ge(s_hh, e + 1)
                for f in range(FC):
                    o = pe.transpose(psX[:, 0, f * P:(f + 1) * P], hh[:, f * P:(f + 1) * P], ident[:, :])
                o.then_inc(s_hT, 1)

            def output_mm(e, halves=range(2)):
                for h in halves:
                    if h == 0:
                        pe.wait_ge(s_hlo, e + 1)
                    c = 4 + h
                    pe.wait_ge(s_ewlo, PIECES * e + c + 1)
                    for f in range(FC):
                        cols = slice(f * TB, (f + 1) * TB)
                        o = three(psY[:, h, :], hT_hi[:, f, :], hT_lo[:, f, :], ew_hi[:, c % 3, cols],
                                  ew_lo[:, c % 3, cols], f == 0, f == FC - 1)
                    o.then_inc(s_ewu, 1)

            def token_sums(j):
                pe.wait_ge(s_sum, KC * (j + 1) + 1)
                pe.wait_ge(s_vq, 16 * j + 16 + 1)
                pe.wait_ge(s_go, 16 * j + 8 + 2)
                for i, t in enumerate((y_sum, q_sum)):
                    for s in range(NT):
                        o = pe.matmul(psA[:, 0, i * NT + s:i * NT + s + 1], t[:, s * P:(s + 1) * P],
                                      ones[:, 0:1], start=True, stop=True)
                o.then_inc(s_smm, 1)

            def token_turn(j):
                pe.wait_ge(s_col, CS * j + 7)
                for t in range(NT):
                    o = pe.transpose(psA[:, 1, t * P:(t + 1) * P], tok6[:, t, :], ident[:, :])
                o.then_inc(s_tT, 1)

            def shifts(j, i):
                if i == 0:
                    pe.wait_ge(s_t6, j + 1)
                for m in (2 * i, 2 * i + 1):
                    if i > 0:
                        pe.wait_ge(s_z, 2 * KC * j + 4 * i - 3 + m % 2)
                    pe.matmul(psA[:, m % 2, :], ln6T[:, m, :], tok6T[:, :], start=True, stop=True
                              ).then_inc(s_sh, 1)

            def run(j, e0, last):
                with_e = e0 is not None
                if with_e:
                    wait_alone(pe, s_xlo, 4 * j)

                def qvg(mm):
                    e = None if not with_e else e0 + mm
                    qvg_proj(j, mm, 0)
                    qvg_proj(j, mm, 1)
                    if with_e:
                        hidden_turn(e)
                    qvg_proj(j, mm, 2)
                    if with_e:
                        output_mm(e)
                        gather_turn(e + 1)
                    qvg_proj(j, mm, 3)
                    qvg_proj(j, mm, 4)
                    qvg_proj(j, mm, 5)
                    if with_e:
                        hidden_mm(e + 1)

                each_qvg(pe, qvg)
                e = None if not with_e else e0 + 4
                token_sums(j)
                if with_e:
                    hidden_turn(e)
                    output_mm(e, (0,))
                token_turn(j)
                if with_e:
                    gather_turn(e + 1)
                shifts(j, 0)
                if with_e:
                    output_mm(e, (1,))
                for i in range(1, 4):
                    shifts(j, i)
                    if with_e:
                        hidden_mm(e + 1, (i - 1,))
                if with_e:
                    hidden_mm(e + 1, (3,))

                def outp(mm, loads, splits, merge):
                    out_proj(j, mm, 0)
                    if with_e:
                        e = e0 + 5 + mm
                        hidden_turn(e)
                    if not last:
                        pe.wait_ge(s_xnl, 16 * (4 * j + mm + 1))
                        for k in range(KC):
                            o = pe.transpose(psH[:, k // 4, (k % 4) * P:(k % 4 + 1) * P],
                                             xn[:, k * P:(k + 1) * P], ident[:, :])
                        o.then_inc(s_xT, 1)
                    out_proj(j, mm, 1, (0,))
                    if with_e:
                        output_mm(e)
                        gather_turn(e + 1)
                    out_proj(j, mm, 1, (1,))
                    if with_e:
                        hidden_mm(e + 1)

                def between(i):
                    if i == 0:
                        pe.wait_ge(s_lf, 1 + SLOTS // 8)
                        pe.transpose(psX[:, 0, 0:SEL], lf[:, :], ident[0:SEL, 0:SEL]).then_inc(s_lfT, 1)
                    elif i == 1:
                        pe.wait_ge(s_ix, 5)
                        gather_turn(0)
                    else:
                        pe.wait_ge(s_xlo, NT)
                        hidden_mm(0)

                each_out(pe, not with_e, last, outp, between)

            phases(pe, run)
            hidden_turn(experts - 1)
            output_mm(experts - 1)


def kernel(L0_attn_x, L0_attn_Wq, L0_attn_Wv, L0_attn_Wg, L0_attn_Wo, L0_attn_beta, L0_attn_ln_g,
           L0_attn_ln_b, L0_ffn_router_w, L0_ffn_w1, L0_ffn_v1, L0_ffn_w2):
    import concourse.bacc as bacc
    from concourse.bass_utils import run_bass_kernel_spmd

    B, S, D = L0_attn_x.shape
    E, F, _ = L0_ffn_w1.shape
    K, H = D // P, L0_attn_beta.shape[0]
    NB = B * S // TB

    cut = lambda w: np.asarray(w).reshape(K, P, K, P).transpose(2, 1, 0, 3)
    vqg = np.stack([cut(L0_attn_Wv), cut(L0_attn_Wq), cut(L0_attn_Wg)], axis=1).reshape(3 * K, P, K * P)
    steps = np.concatenate([vqg, cut(L0_attn_Wo).reshape(K, P, K * P)])
    steps = np.ascontiguousarray(np.concatenate([steps, steps[:4]]))
    up = np.stack([np.asarray(L0_ffn_w1), np.asarray(L0_ffn_v1)], axis=1)
    up = up.reshape(E, 2, F, 4, K // 4, P).transpose(0, 3, 5, 4, 1, 2).reshape(E, 4, P, -1)
    down = np.asarray(L0_ffn_w2).reshape(E, F // P, P, 2, D // 2).transpose(0, 3, 2, 1, 4).reshape(E, 2, P, -1)
    ew = np.concatenate([up, down], axis=1)
    router = np.zeros((P, K, SEL), np.float32)
    router[:, :, :E] = np.asarray(L0_ffn_router_w).reshape(E, K, P).transpose(2, 1, 0)
    per_part = lambda v: np.ascontiguousarray(np.asarray(v).reshape(K, P).T)
    beta = np.ascontiguousarray(np.repeat(np.asarray(L0_attn_beta), D // H).reshape(K, P).T)
    arrays = {
        "x": np.ascontiguousarray(np.asarray(L0_attn_x).reshape(B * S, D)), "proj_w": steps, "ew": ew,
        "router": router, "beta": beta, "ln_g": per_part(L0_attn_ln_g), "ln_b": per_part(L0_attn_ln_b),
    }
    nc = bacc.Bacc("TRN2", target_bir_lowering=False, num_devices=1)
    aps = {n: nc.dram_tensor(n + "_dram", a.shape, F32, kind="ExternalInput").ap() for n, a in arrays.items()}
    out = nc.dram_tensor("out_dram", (B * S, D), F32, kind="ExternalOutput").ap()
    build(nc, aps["x"], aps["proj_w"], aps["ew"], aps["router"], aps["beta"], aps["ln_g"], aps["ln_b"], out,
          B, S, E)
    r = run_bass_kernel_spmd(nc, [{n + "_dram": a for n, a in arrays.items()}], core_ids=[0])
    return r.results[0]["out_dram"].reshape(B, S, D)
```
